# Optimizing a Trainium2 kernel written in Bass

```python
import numpy as np
import jax
import jax.numpy as jnp

def _softmax(x, axis=-1):
    return jax.nn.softmax(x, axis=axis)

def _gelu(x):
    return jax.nn.gelu(x, approximate=True)

def _silu(x):
    return jax.nn.silu(x)

def _sigmoid(x):
    return jax.nn.sigmoid(x)

def _layernorm(x, axis=-1, eps=1e-05):
    m = jnp.mean(x, axis=axis, keepdims=True)
    v = jnp.var(x, axis=axis, keepdims=True)
    return (x - m) / jnp.sqrt(v + eps)

def _scatter_add(tgt, idx, src, axis=0):
    return tgt.at[idx].add(src)

def _segment_sum(src, seg, n):
    return jax.ops.segment_sum(src, seg, n)
kernel_name = 'mk_macaron_d2_jaxref_r8_4ce686'

def setup_inputs(seed: int=0):
    np.random.seed(seed)
    _w = jnp.asarray

    def _L0_attn_setup():
        import jax, jax.numpy as jnp
        import numpy as np
        import math
        B, T, C = (2, 256, 128)
        H, L = (16, 64)
        DH = C // H
        DHE = DH // 2
        THETA = 10000.0

        def _rope_cache(t, dim):
            inv_freq = 1.0 / THETA ** (jnp.arange(0, dim, 2, dtype=jnp.float32) / dim)
            freqs = jnp.arange(t, dtype=jnp.float32)[:, None] * inv_freq[None, :]
            emb = jnp.concatenate((freqs, freqs), axis=-1)
            return (jnp.cos(emb), jnp.sin(emb))

        def _apply_rope(x, cos, sin):
            x1 = x[..., 0::2]
            x2 = x[..., 1::2]
            rot = jnp.stack((-x2, x1), axis=-1).reshape(x.shape)
            return x * cos[None, None] + rot * sin[None, None]
        key = jax.random.key(seed)
        ks = jax.random.split(key, 10)
        s = 0.02
        return {'x': jax.random.normal(ks[0], (B, T, C), jnp.float32), 'Wq_down': jax.random.normal(ks[1], (C, H * L), jnp.float32) * s, 'Wk_down': jax.random.normal(ks[2], (C, H * L), jnp.float32) * s, 'Wv_down': jax.random.normal(ks[3], (C, H * L), jnp.float32) * s, 'Wq_up_c': jax.random.normal(ks[4], (L, DHE), jnp.float32) * s, 'Wq_up_e': jax.random.normal(ks[5], (L, DHE), jnp.float32) * s, 'Wk_up_c': jax.random.normal(ks[6], (L, DHE), jnp.float32) * s, 'Wk_up_e': jax.random.normal(ks[7], (L, DHE), jnp.float32) * s, 'Wv_up': jax.random.normal(ks[8], (L, DH), jnp.float32) * s, 'Wc': jax.random.normal(ks[9], (C, C), jnp.float32) * s}
    _L0_attn_in = _L0_attn_setup()

    def _L0_ffn_setup():
        import jax, jax.numpy as jnp
        import numpy as np
        B, N, D = (4, 1024, 128)
        HEADS, DH = (8, 64)
        HID = HEADS * DH
        WIN = 128
        NQ, NKV = (128, 256)
        EPS, N_ITERS, FETCH_K = (1.0, 50, 9.0 / 8.0)
        SCALE = DH ** (-0.5)

        def rmsnorm(x, gamma):
            norm = jnp.maximum(jnp.linalg.norm(x, axis=-1, keepdims=True), 1e-12)
            return x / norm * x.shape[-1] ** 0.5 * gamma

        def coor_descent(s, k):
            logk = jnp.log(jnp.asarray(k, s.dtype))

            def body(_, ab):
                a, b = ab
                a = EPS * (logk - jax.nn.logsumexp((s + b) / EPS, axis=-1, keepdims=True))
                b = -jax.nn.relu(s + a)
                return (a, b)
            a, b = jax.lax.fori_loop(0, N_ITERS, body, (jnp.zeros_like(s[..., :1]), -s))
            return jnp.exp((s + a + b) / EPS)

        def route(x, routing_token, num_tokens):
            s = jnp.einsum('bnd,d->bn', x, routing_token)
            k = min(num_tokens * FETCH_K, x.shape[1])
            scores = coor_descent(s, k)
            sel_scores, sel_idx = jax.lax.top_k(scores, num_tokens)
            sel_scores = sel_scores + jax.lax.stop_gradient(1.0 - sel_scores)
            return (sel_scores, sel_idx)

        def light_local_attn(x, gamma, wq, wkv, wo):
            b, n, d = x.shape
            xn = rmsnorm(x, gamma)
            q = xn @ wq
            k, v = jnp.split(xn @ wkv, 2, axis=-1)

            def win(t):
                return t.reshape(b, n // WIN, WIN, HEADS, DH).transpose(0, 1, 3, 2, 4)
            q, k, v = (win(q) * SCALE, win(k), win(v))
            attn = jax.nn.softmax(jnp.einsum('bwhid,bwhjd->bwhij', q, k), axis=-1)
            out = jnp.einsum('bwhij,bwhjd->bwhid', attn, v)
            out = out.transpose(0, 1, 3, 2, 4).reshape(b, n, HID)
            return out @ wo

        def heavy_attn(xq, context, scores_kv, gamma, wq, wkv_t, wo):
            b, nq, d = xq.shape
            nkv = context.shape[1]
            xqn = rmsnorm(xq, gamma)
            ctx = rmsnorm(context, gamma)[:, None]
            q = (xqn @ wq).reshape(b, nq, HEADS, DH).transpose(0, 2, 1, 3) * SCALE
            kvw = wkv_t.reshape(1, HEADS, 2 * DH, d)
            kv = jnp.einsum('rhdi,brni->brhnd', kvw, ctx)
            k, v = jnp.split(kv, 2, axis=-1)
            v = v * scores_kv[:, None, None, :, None]
            k = k.reshape(b, HEADS, nkv, DH)
            v = v.reshape(b, HEADS, nkv, DH)
            attn = jax.nn.softmax(jnp.einsum('bhid,bhjd->bhij', q, k), axis=-1)
            out = jnp.einsum('bhij,bhjd->bhid', attn, v)
            out = out.transpose(0, 2, 1, 3).reshape(b, nq, HID)
            return out @ wo
        key = jax.random.key(seed)
        ks = jax.random.split(key, 10)
        lin = lambda k, shape, fan: jax.random.normal(k, shape, jnp.float32) * fan ** (-0.5)
        return dict(x=jax.random.normal(ks[0], (B, N, D), jnp.float32), gamma_light=jnp.ones((D,), jnp.float32), wq_light=lin(ks[1], (D, HID), D), wkv_light=lin(ks[2], (D, 2 * HID), D), wo_light=lin(ks[3], (HID, D), HID), q_routing_token=jax.random.normal(ks[4], (D,), jnp.float32), kv_routing_token=jax.random.normal(ks[5], (D,), jnp.float32), gamma_heavy=jnp.ones((D,), jnp.float32), wq_heavy=lin(ks[6], (D, HID), D), wkv_heavy=lin(ks[7], (2 * HID, D), D), wo_heavy=lin(ks[8], (HID, D), HID))
    _L0_ffn_in = _L0_ffn_setup()

    def _L1_attn_setup():
        import jax, jax.numpy as jnp
        import numpy as np
        import math
        DIM = 128
        NUM_HEADS = 16
        HEAD_DIM = DIM // NUM_HEADS
        LOGIT_SCALE_MAX = math.log(1.0 / 0.01)
        EPS = 1e-12

        def _l2_normalize(t):
            n = jnp.sqrt(jnp.sum(t * t, axis=-1, keepdims=True))
            return t / jnp.maximum(n, EPS)
        key = jax.random.key(seed)
        ks = jax.random.split(key, 4)
        L, N, C = (128, 8, DIM)
        scale = HEAD_DIM ** (-0.5)
        x = jax.random.normal(ks[0], (L, N, C), dtype=jnp.float32)
        in_proj_weight = jax.random.normal(ks[1], (3 * C, C), dtype=jnp.float32) * scale
        in_proj_bias = jnp.zeros((3 * C,), dtype=jnp.float32)
        logit_scale = jnp.full((NUM_HEADS, 1, 1), math.log(10.0), dtype=jnp.float32)
        head_scale = jnp.ones((NUM_HEADS, 1, 1), dtype=jnp.float32)
        out_w = jax.random.normal(ks[2], (C, C), dtype=jnp.float32) * C ** (-0.5)
        out_b = jax.random.normal(ks[3], (C,), dtype=jnp.float32) * 0.01
        return {'x': x, 'in_proj_weight': in_proj_weight, 'in_proj_bias': in_proj_bias, 'logit_scale': logit_scale, 'head_scale': head_scale, 'out_w': out_w, 'out_b': out_b}
    _L1_attn_in = _L1_attn_setup()

    def _L1_ffn_setup():
        import jax, jax.numpy as jnp
        import numpy as np
        E, K, H, F = (64, 6, 128, 64)
        SHARED_F = 256
        B, S = (1, 256)
        T = B * S
        CAP = 2 * ((T * K + E - 1) // E)
        key = jax.random.key(seed)
        ks = jax.random.split(key, 6)
        s = 0.05
        return {'hidden_states': jax.random.normal(ks[0], (B, S, H), jnp.float32), 'router_weight': jax.random.normal(ks[1], (E, H), jnp.float32) * s, 'expert_bias': jnp.zeros((E,), jnp.float32), 'w1': jax.random.normal(ks[2], (E, H, F), jnp.float32) * s, 'w2': jax.random.normal(ks[3], (E, F, H), jnp.float32) * s, 'sw1': jax.random.normal(ks[4], (SHARED_F, H), jnp.float32) * s, 'sw2': jax.random.normal(ks[5], (H, SHARED_F), jnp.float32) * s}
    _L1_ffn_in = _L1_ffn_setup()
    _d = {'L0_attn_x': _L0_attn_in['x'], 'L0_attn_Wq_down': _L0_attn_in['Wq_down'], 'L0_attn_Wk_down': _L0_attn_in['Wk_down'], 'L0_attn_Wv_down': _L0_attn_in['Wv_down'], 'L0_attn_Wq_up_c': _L0_attn_in['Wq_up_c'], 'L0_attn_Wq_up_e': _L0_attn_in['Wq_up_e'], 'L0_attn_Wk_up_c': _L0_attn_in['Wk_up_c'], 'L0_attn_Wk_up_e': _L0_attn_in['Wk_up_e'], 'L0_attn_Wv_up': _L0_attn_in['Wv_up'], 'L0_attn_Wc': _L0_attn_in['Wc'], 'L0_ffn_gamma_light': _L0_ffn_in['gamma_light'], 'L0_ffn_wq_light': _L0_ffn_in['wq_light'], 'L0_ffn_wkv_light': _L0_ffn_in['wkv_light'], 'L0_ffn_wo_light': _L0_ffn_in['wo_light'], 'L0_ffn_q_routing_token': _L0_ffn_in['q_routing_token'], 'L0_ffn_kv_routing_token': _L0_ffn_in['kv_routing_token'], 'L0_ffn_gamma_heavy': _L0_ffn_in['gamma_heavy'], 'L0_ffn_wq_heavy': _L0_ffn_in['wq_heavy'], 'L0_ffn_wkv_heavy': _L0_ffn_in['wkv_heavy'], 'L0_ffn_wo_heavy': _L0_ffn_in['wo_heavy'], 'L1_attn_in_proj_weight': _L1_attn_in['in_proj_weight'], 'L1_attn_in_proj_bias': _L1_attn_in['in_proj_bias'], 'L1_attn_logit_scale': _L1_attn_in['logit_scale'], 'L1_attn_head_scale': _L1_attn_in['head_scale'], 'L1_attn_out_w': _L1_attn_in['out_w'], 'L1_attn_out_b': _L1_attn_in['out_b'], 'L1_ffn_router_weight': _L1_ffn_in['router_weight'], 'L1_ffn_expert_bias': _L1_ffn_in['expert_bias'], 'L1_ffn_w1': _L1_ffn_in['w1'], 'L1_ffn_w2': _L1_ffn_in['w2'], 'L1_ffn_sw1': _L1_ffn_in['sw1'], 'L1_ffn_sw2': _L1_ffn_in['sw2']}
    _x0 = _d['L0_attn_x']
    _d['L0_attn_x'] = jax.random.normal(jax.random.fold_in(jax.random.key(seed), 1), (16, 512, 128), dtype=_x0.dtype)
    del _x0
    return _d

def reference(L0_attn_x, L0_attn_Wq_down, L0_attn_Wk_down, L0_attn_Wv_down, L0_attn_Wq_up_c, L0_attn_Wq_up_e, L0_attn_Wk_up_c, L0_attn_Wk_up_e, L0_attn_Wv_up, L0_attn_Wc, L0_ffn_gamma_light, L0_ffn_wq_light, L0_ffn_wkv_light, L0_ffn_wo_light, L0_ffn_q_routing_token, L0_ffn_kv_routing_token, L0_ffn_gamma_heavy, L0_ffn_wq_heavy, L0_ffn_wkv_heavy, L0_ffn_wo_heavy, L1_attn_in_proj_weight, L1_attn_in_proj_bias, L1_attn_logit_scale, L1_attn_head_scale, L1_attn_out_w, L1_attn_out_b, L1_ffn_router_weight, L1_ffn_expert_bias, L1_ffn_w1, L1_ffn_w2, L1_ffn_sw1, L1_ffn_sw2):

    def _L0_attn_ref(x, Wq_down, Wk_down, Wv_down, Wq_up_c, Wq_up_e, Wk_up_c, Wk_up_e, Wv_up, Wc):
        import jax, jax.numpy as jnp
        import numpy as np
        import math
        B, T, C = (2, 256, 128)
        H, L = (16, 64)
        DH = C // H
        DHE = DH // 2
        THETA = 10000.0

        def _rope_cache(t, dim):
            inv_freq = 1.0 / THETA ** (jnp.arange(0, dim, 2, dtype=jnp.float32) / dim)
            freqs = jnp.arange(t, dtype=jnp.float32)[:, None] * inv_freq[None, :]
            emb = jnp.concatenate((freqs, freqs), axis=-1)
            return (jnp.cos(emb), jnp.sin(emb))

        def _apply_rope(x, cos, sin):
            x1 = x[..., 0::2]
            x2 = x[..., 1::2]
            rot = jnp.stack((-x2, x1), axis=-1).reshape(x.shape)
            return x * cos[None, None] + rot * sin[None, None]
        b, t, c = x.shape
        q_lat = (x @ Wq_down).reshape(b, t, H, L)
        k_lat = (x @ Wk_down).reshape(b, t, H, L)
        v_lat = (x @ Wv_down).reshape(b, t, H, L)
        q_c = jnp.einsum('bthl,ld->bhtd', q_lat, Wq_up_c)
        q_e = jnp.einsum('bthl,ld->bhtd', q_lat, Wq_up_e)
        k_c = jnp.einsum('bthl,ld->bhtd', k_lat, Wk_up_c)
        k_e = jnp.einsum('bthl,ld->bhtd', k_lat, Wk_up_e)
        v = jnp.einsum('bthl,ld->bhtd', v_lat, Wv_up)
        cos, sin = _rope_cache(t, DHE)
        q = jnp.concatenate([q_c, _apply_rope(q_e, cos, sin)], axis=-1)
        k = jnp.concatenate([k_c, _apply_rope(k_e, cos, sin)], axis=-1)
        scale = 1.0 / math.sqrt(DH)
        scores = jnp.einsum('bhqd,bhkd->bhqk', q, k) * scale
        causal = jnp.tril(jnp.ones((t, t), dtype=bool))
        scores = jnp.where(causal[None, None], scores, -jnp.inf)
        att = jax.nn.softmax(scores, axis=-1)
        y = jnp.einsum('bhqk,bhkd->bhqd', att, v)
        y = y.transpose(0, 2, 1, 3).reshape(b, t, c)
        return y @ Wc

    def _L0_ffn_ref(x, gamma_light, wq_light, wkv_light, wo_light, q_routing_token, kv_routing_token, gamma_heavy, wq_heavy, wkv_heavy, wo_heavy):
        import jax, jax.numpy as jnp
        import numpy as np
        B, N, D = (4, 1024, 128)
        HEADS, DH = (8, 64)
        HID = HEADS * DH
        WIN = 128
        NQ, NKV = (128, 256)
        EPS, N_ITERS, FETCH_K = (1.0, 50, 9.0 / 8.0)
        SCALE = DH ** (-0.5)

        def rmsnorm(x, gamma):
            norm = jnp.maximum(jnp.linalg.norm(x, axis=-1, keepdims=True), 1e-12)
            return x / norm * x.shape[-1] ** 0.5 * gamma

        def coor_descent(s, k):
            logk = jnp.log(jnp.asarray(k, s.dtype))

            def body(_, ab):
                a, b = ab
                a = EPS * (logk - jax.nn.logsumexp((s + b) / EPS, axis=-1, keepdims=True))
                b = -jax.nn.relu(s + a)
                return (a, b)
            a, b = jax.lax.fori_loop(0, N_ITERS, body, (jnp.zeros_like(s[..., :1]), -s))
            return jnp.exp((s + a + b) / EPS)

        def route(x, routing_token, num_tokens):
            s = jnp.einsum('bnd,d->bn', x, routing_token)
            k = min(num_tokens * FETCH_K, x.shape[1])
            scores = coor_descent(s, k)
            sel_scores, sel_idx = jax.lax.top_k(scores, num_tokens)
            sel_scores = sel_scores + jax.lax.stop_gradient(1.0 - sel_scores)
            return (sel_scores, sel_idx)

        def light_local_attn(x, gamma, wq, wkv, wo):
            b, n, d = x.shape
            xn = rmsnorm(x, gamma)
            q = xn @ wq
            k, v = jnp.split(xn @ wkv, 2, axis=-1)

            def win(t):
                return t.reshape(b, n // WIN, WIN, HEADS, DH).transpose(0, 1, 3, 2, 4)
            q, k, v = (win(q) * SCALE, win(k), win(v))
            attn = jax.nn.softmax(jnp.einsum('bwhid,bwhjd->bwhij', q, k), axis=-1)
            out = jnp.einsum('bwhij,bwhjd->bwhid', attn, v)
            out = out.transpose(0, 1, 3, 2, 4).reshape(b, n, HID)
            return out @ wo

        def heavy_attn(xq, context, scores_kv, gamma, wq, wkv_t, wo):
            b, nq, d = xq.shape
            nkv = context.shape[1]
            xqn = rmsnorm(xq, gamma)
            ctx = rmsnorm(context, gamma)[:, None]
            q = (xqn @ wq).reshape(b, nq, HEADS, DH).transpose(0, 2, 1, 3) * SCALE
            kvw = wkv_t.reshape(1, HEADS, 2 * DH, d)
            kv = jnp.einsum('rhdi,brni->brhnd', kvw, ctx)
            k, v = jnp.split(kv, 2, axis=-1)
            v = v * scores_kv[:, None, None, :, None]
            k = k.reshape(b, HEADS, nkv, DH)
            v = v.reshape(b, HEADS, nkv, DH)
            attn = jax.nn.softmax(jnp.einsum('bhid,bhjd->bhij', q, k), axis=-1)
            out = jnp.einsum('bhij,bhjd->bhid', attn, v)
            out = out.transpose(0, 2, 1, 3).reshape(b, nq, HID)
            return out @ wo
        b = x.shape[0]
        light_out = light_local_attn(x, gamma_light, wq_light, wkv_light, wo_light)
        scores_q, idx_q = route(x, q_routing_token, NQ)
        scores_kv, idx_kv = route(x, kv_routing_token, NKV)
        routed_q = jnp.take_along_axis(x, idx_q[..., None], axis=1)
        routed_kv = jnp.take_along_axis(x, idx_kv[..., None], axis=1)
        routed_out = heavy_attn(routed_q, routed_kv, scores_kv, gamma_heavy, wq_heavy, wkv_heavy, wo_heavy)
        routed_out = routed_out * scores_q[..., None]
        heavy_out = jnp.zeros_like(x).at[jnp.arange(b)[:, None], idx_q].set(routed_out)
        return light_out + heavy_out

    def _L1_attn_ref(x, in_proj_weight, in_proj_bias, logit_scale, head_scale, out_w, out_b):
        import jax, jax.numpy as jnp
        import numpy as np
        import math
        DIM = 128
        NUM_HEADS = 16
        HEAD_DIM = DIM // NUM_HEADS
        LOGIT_SCALE_MAX = math.log(1.0 / 0.01)
        EPS = 1e-12

        def _l2_normalize(t):
            n = jnp.sqrt(jnp.sum(t * t, axis=-1, keepdims=True))
            return t / jnp.maximum(n, EPS)
        L, N, C = x.shape
        H, hd = (NUM_HEADS, HEAD_DIM)
        qkv = x @ in_proj_weight.T + in_proj_bias
        q, k, v = jnp.split(qkv, 3, axis=-1)

        def to_heads(t):
            return t.reshape(L, N, H, hd).transpose(1, 2, 0, 3)
        q, k, v = (to_heads(q), to_heads(k), to_heads(v))
        ls = jnp.exp(jnp.minimum(logit_scale, LOGIT_SCALE_MAX))
        attn = jnp.einsum('nhld,nhmd->nhlm', _l2_normalize(q), _l2_normalize(k)) * ls
        attn = jax.nn.softmax(attn, axis=-1)
        o = jnp.einsum('nhlm,nhmd->nhld', attn, v)
        o = o * head_scale
        o = o.transpose(2, 0, 1, 3).reshape(L, N, C)
        return o @ out_w.T + out_b

    def _L1_ffn_ref(hidden_states, router_weight, expert_bias, w1, w2, sw1, sw2):
        import jax, jax.numpy as jnp
        import numpy as np
        E, K, H, F = (64, 6, 128, 64)
        SHARED_F = 256
        B, S = (1, 256)
        T = B * S
        CAP = 2 * ((T * K + E - 1) // E)
        b, s, h = hidden_states.shape
        x = hidden_states.reshape(-1, h)
        t = x.shape[0]
        logits = x @ router_weight.T
        scores = jax.nn.sigmoid(logits)
        _, top_idx = jax.lax.top_k(scores + expert_bias[None, :], K)
        top_scores = jnp.take_along_axis(scores, top_idx, axis=1)
        probs = top_scores / (jnp.sum(top_scores, axis=-1, keepdims=True) + 1e-20)
        flat_e = top_idx.reshape(-1)
        order = jnp.argsort(flat_e)
        sorted_e = flat_e[order]
        token_of = order // K
        counts = jnp.bincount(flat_e, length=E)
        offsets = jnp.cumsum(counts) - counts
        pos = jnp.arange(t * K) - offsets[sorted_e]
        valid = pos < CAP
        slot = jnp.where(valid, sorted_e * CAP + pos, E * CAP)
        xs = jnp.zeros((E * CAP + 1, h), x.dtype).at[slot].set(x[token_of])
        xs = xs[:-1].reshape(E, CAP, h)
        hmid = jax.nn.gelu(jnp.einsum('ech,ehf->ecf', xs, w1), approximate=True)
        y = jnp.einsum('ecf,efh->ech', hmid, w2).reshape(E * CAP, h)
        pair_w = jnp.where(valid, probs.reshape(-1)[order], 0.0)
        y_pair = y[jnp.minimum(slot, E * CAP - 1)] * pair_w[:, None]
        out = jnp.zeros((t, h), x.dtype).at[token_of].add(y_pair)
        shared = jax.nn.gelu(x @ sw1.T, approximate=True) @ sw2.T
        return (out + shared).reshape(b, s, h)
    x = L0_attn_x
    x = x + 0.5 * _L0_ffn_ref(_layernorm(x, axis=-1), L0_ffn_gamma_light, L0_ffn_wq_light, L0_ffn_wkv_light, L0_ffn_wo_light, L0_ffn_q_routing_token, L0_ffn_kv_routing_token, L0_ffn_gamma_heavy, L0_ffn_wq_heavy, L0_ffn_wkv_heavy, L0_ffn_wo_heavy)
    x = x + _L0_attn_ref(_layernorm(x, axis=-1), L0_attn_Wq_down, L0_attn_Wk_down, L0_attn_Wv_down, L0_attn_Wq_up_c, L0_attn_Wq_up_e, L0_attn_Wk_up_c, L0_attn_Wk_up_e, L0_attn_Wv_up, L0_attn_Wc)
    x = x + 0.5 * _L0_ffn_ref(_layernorm(x, axis=-1), L0_ffn_gamma_light, L0_ffn_wq_light, L0_ffn_wkv_light, L0_ffn_wo_light, L0_ffn_q_routing_token, L0_ffn_kv_routing_token, L0_ffn_gamma_heavy, L0_ffn_wq_heavy, L0_ffn_wkv_heavy, L0_ffn_wo_heavy)
    x = x + 0.5 * _L1_ffn_ref(_layernorm(x, axis=-1), L1_ffn_router_weight, L1_ffn_expert_bias, L1_ffn_w1, L1_ffn_w2, L1_ffn_sw1, L1_ffn_sw2)
    x = x + _L1_attn_ref(_layernorm(x, axis=-1), L1_attn_in_proj_weight, L1_attn_in_proj_bias, L1_attn_logit_scale, L1_attn_head_scale, L1_attn_out_w, L1_attn_out_b)
    x = x + 0.5 * _L1_ffn_ref(_layernorm(x, axis=-1), L1_ffn_router_weight, L1_ffn_expert_bias, L1_ffn_w1, L1_ffn_w2, L1_ffn_sw1, L1_ffn_sw2)
    return x

_drawn_inputs = setup_inputs


def setup_inputs(seed=0):
    import zlib

    import numpy as np

    out = dict(_drawn_inputs(seed))
    spreads = {'L0_ffn_gamma_light': (1.0, 0.2),
     'L0_ffn_gamma_heavy': (1.0, 0.2),
     'L1_attn_in_proj_bias': (0.0, 0.1),
     'L1_attn_logit_scale': (2.3025851249694824, 0.2),
     'L1_attn_head_scale': (1.0, 0.2),
     'L1_ffn_expert_bias': (0.0, 0.42)}
    factors = {'L0_attn_Wq_down': 8.0,
     'L0_attn_Wk_down': 8.0,
     'L0_attn_Wv_down': 8.0,
     'L0_attn_Wq_up_c': 8.0,
     'L0_attn_Wq_up_e': 8.0,
     'L0_attn_Wk_up_c': 8.0,
     'L0_attn_Wk_up_e': 8.0,
     'L0_attn_Wv_up': 8.0,
     'L0_attn_Wc': 8.0,
     'L1_attn_out_b': 23.362,
     'L1_ffn_router_weight': 3.483,
     'L1_ffn_w1': 3.535,
     'L1_ffn_w2': 3.403}
    for name, (base, spread) in spreads.items():
        noise = np.random.default_rng([zlib.crc32(name.encode()), seed]).standard_normal(out[name].shape)
        drawn = base * np.exp(spread * noise) if base else spread * noise
        out[name] = jnp.asarray(drawn.astype(out[name].dtype))
    for name, factor in factors.items():
        out[name] = (out[name] * factor).astype(out[name].dtype)
    return out
```

```python
from contextlib import ExitStack

import numpy as np
import concourse.bass as bass
from concourse import mybir

F32 = mybir.dt.float32
BF16 = mybir.dt.bfloat16
I32 = mybir.dt.int32
U32 = mybir.dt.uint32
ALU = mybir.AluOpType
ACT = mybir.ActivationFunctionType
X_AX = mybir.AxisListType.X

P = 128
B, T, C = 16, 512, 128
TOK = B * T
NT = TOK // P
TPB = T // P
LN_EPS = 1e-5

HEADS, DH = 8, 64
PAIRS = HEADS // 2
HID = HEADS * DH
NQ, NKV = 128, 256
ITERS = 50
FETCH = 9.0 / 8.0
ROWS = 48
KV0 = 32
NORM_EPS = 1e-12


class Arena:

    def __init__(self, nc, ctx, tag):
        self.nc, self.ctx, self.tag, self.sems = nc, ctx, tag, []
        ctx.callback(self.close)

    def close(self):
        if self.sems:
            self.nc.clear_and_free_semaphores(self.sems)
            self.nc.all_engine_barrier()

    def sb(self, name, shape, dt=F32):
        return self.ctx.enter_context(self.nc.sbuf_tensor(f"{self.tag}_{name}", shape, dt))

    def ps(self, name, shape, dt=F32):
        return self.ctx.enter_context(self.nc.psum_tensor(f"{self.tag}_{name}", shape, dt))

    def sem(self, name):
        self.sems.append(self.nc.alloc_semaphore(f"{self.tag}_{name}"))
        return self.sems[-1]


def past(i, n):
    return not isinstance(i, int) or i >= n


class Chain:

    def __init__(self, eng, sem):
        self.eng, self.sem, self.n = eng, sem, 0

    def step(self, ins):
        self.n += 1
        ins.then_inc(self.sem, 1)
        self.eng.wait_ge(self.sem, self.n)


def router_prologue(nc, tag, x, scale_a, shift_b, s_rows, s_scr, rtok_dram, ident):
    CH = 16
    NCH = NT // CH
    with ExitStack() as ctx:
        A = Arena(nc, ctx, tag)
        rtok = A.sb("rtok", [P, 2, C])
        cen = A.sb("cen", [P, 2, CH, C])
        sq = A.sb("sq", [P, CH, C])
        prod = A.sb("prod", [P, 2, CH, C])
        mean = A.sb("mean", [P, NT])
        ssq = A.sb("ssq", [P, NT])
        dots = A.sb("dots", [P, 2, NT])
        var = A.sb("var", [P, NT])
        std = A.sb("std", [P, NT])
        nrm = A.sb("nrm", [P, NT])
        t1 = A.sb("t1", [P, NT])
        sT = A.sb("sT", [P, P])
        psT = A.ps("psT", [P, P])
        rtok_in = A.sem("rtok_in")
        cen_ready = A.sem("cen_ready")
        sq_ready = A.sem("sq_ready")
        prod_ready = A.sem("prod_ready")
        prod_used = A.sem("prod_used")
        dve_step = A.sem("dve_step")
        var_ready = A.sem("var_ready")
        std_ready = A.sem("std_ready")
        nrm_ready = A.sem("nrm_ready")
        dots_ready = A.sem("dots_ready")
        sT_ps = A.sem("sT_ps")
        sT_sb = A.sem("sT_sb")
        s_out = A.sem("s_out")
        s_in = A.sem("s_in")
        zeroed = A.sem("zeroed")
        block = ctx.enter_context(nc.Block())

        @block.sync
        def _(sp):
            sp.dma_start(rtok[:], rtok_dram.rearrange("(a r) c -> a r c", a=1).broadcast_to([P, 2, C])).then_inc(rtok_in, 16)
            sp.wait_ge(sT_sb, 1)
            sp.dma_start(s_scr, sT[:]).then_inc(s_out, 16)
            sp.wait_ge(s_out, 16)
            sp.wait_ge(zeroed, 1)
            rows = s_scr.rearrange("(r b j) t -> r b (j t)", r=2, b=B)
            sp.dma_start(s_rows[0:B, :], rows[0]).then_inc(s_in, 16)
            sp.dma_start(s_rows[KV0:KV0 + B, :], rows[1]).then_inc(s_in, 16)
            sp.wait_ge(s_in, 32)

        @block.gpsimd
        def _(pool):
            nc.gpsimd.memset(s_rows[:], 0.0).then_inc(zeroed, 1)
            pool.wait_ge(rtok_in, 16)
            for c in range(NCH):
                pool.wait_ge(cen_ready, c + 1)
                if c:
                    pool.wait_ge(prod_used, c)
                for r in range(2):
                    last = nc.gpsimd.tensor_tensor(
                        prod[:, r], cen[:, c % 2], rtok[:, r:r + 1, :].broadcast_to([P, CH, C]), ALU.mult)
                last.then_inc(prod_ready, 1)

        @block.scalar
        def _(act):
            for c in range(NCH):
                act.wait_ge(cen_ready, c + 1)
                if c:
                    act.wait_ge(prod_used, c)
                nc.scalar.activation(sq[:], cen[:, c % 2], ACT.Square).then_inc(sq_ready, 1)
            act.wait_ge(var_ready, 1)
            nc.scalar.activation(std[:], var[:], ACT.Sqrt).then_inc(std_ready, 1)
            nc.scalar.activation(nrm[:], ssq[:], ACT.Sqrt).then_inc(nrm_ready, 1)
            act.wait_ge(sT_ps, 1)
            nc.scalar.copy(sT[:], psT[:]).then_inc(sT_sb, 1)

        @block.tensor
        def _(pe):
            pe.wait_ge(dots_ready, 1)
            nc.tensor.transpose(psT[:], dots[:].rearrange("p r n -> p (r n)"), ident[:]).then_inc(sT_ps, 1)

        @block.vector
        def _(dve):
            ch = Chain(dve, dve_step)

            def sums(c):
                dve.wait_ge(sq_ready, c + 1)
                nc.vector.tensor_reduce(ssq[:, c * CH:(c + 1) * CH], sq[:], X_AX, ALU.add)
                dve.wait_ge(prod_ready, c + 1)
                for r in range(2):
                    last = nc.vector.tensor_reduce(dots[:, r, c * CH:(c + 1) * CH], prod[:, r], X_AX, ALU.add)
                last.then_inc(prod_used, 1)

            for c in range(NCH):
                xs = x[:, c * CH:(c + 1) * CH, :]
                ms = mean[:, c * CH:(c + 1) * CH]
                ch.step(nc.vector.tensor_reduce(ms, xs, X_AX, ALU.add))
                ch.step(nc.vector.tensor_scalar(ms, ms, 1.0 / C, None, ALU.mult))
                nc.vector.tensor_tensor(cen[:, c % 2], xs, ms.rearrange("p (n o) -> p n o", o=1).broadcast_to([P, CH, C]),
                                        ALU.subtract).then_inc(cen_ready, 1)
                if c:
                    sums(c - 1)
            sums(NCH - 1)
            dve.wait_ge(prod_used, NCH)
            nc.vector.tensor_scalar(var[:], ssq[:], 1.0 / C, LN_EPS, ALU.mult, ALU.add).then_inc(var_ready, 1)
            dve.wait_ge(std_ready, 1)
            ch.step(nc.vector.reciprocal(var[:], std[:]))
            for r in range(2):
                last = nc.vector.tensor_tensor(dots[:, r], dots[:, r], var[:], ALU.mult)
            last.then_inc(dots_ready, 1)
            dve.wait_ge(nrm_ready, 1)
            ch.step(nc.vector.tensor_tensor(t1[:], nrm[:], var[:], ALU.mult))
            ch.step(nc.vector.tensor_scalar(t1[:], t1[:], NORM_EPS, None, ALU.max))
            ch.step(nc.vector.reciprocal(t1[:], t1[:]))
            ch.step(nc.vector.tensor_scalar(t1[:], t1[:], float(C) ** 0.5, None, ALU.mult))
            ch.step(nc.vector.tensor_tensor(scale_a[:], t1[:], var[:], ALU.mult))
            ch.step(nc.vector.tensor_tensor(shift_b[:], mean[:], scale_a[:], ALU.mult))
            ch.step(nc.vector.tensor_scalar(shift_b[:], shift_b[:], -1.0, None, ALU.mult))


def light_attention(nc, tag, x, y, scale_a, shift_b, s_rows, scores, logk, w, ident):
    SM = DH ** -0.5
    with ExitStack() as ctx:
        A = Arena(nc, ctx, tag)
        wraw = A.sb("wraw", [P, 3, HID])
        gamma = A.sb("gamma", [P, 1])
        wqkv = A.sb("wqkv", [P, 3, HID])
        wo = A.sb("wo", [P, PAIRS, C])
        xr = A.sb("xr", [P, C])
        xrT = A.sb("xrT", [P, P])
        qz = A.sb("qz", [P, PAIRS, 2, P])
        kT = A.sb("kT", [P, PAIRS, P])
        v = A.sb("v", [P, HEADS, DH + 1])
        mx = A.sb("mx", [P, HEADS])
        ssub = A.sb("ssub", [P, HEADS, P])
        prob = A.sb("prob", [P, HEADS, P])
        probT = A.sb("probT", [P, HEADS, P])
        rec = A.sb("rec", [P, HEADS])
        on = A.sb("on", [P, HEADS, DH])
        oT = A.sb("oT", [P, PAIRS, P])
        tmin = A.sb("tmin", [ROWS, T])
        eexp = A.sb("eexp", [ROWS, T])
        smax = A.sb("smax", [ROWS, 1])
        na = A.sb("na", [ROWS, 1])
        nm = A.sb("nm", [ROWS, 1])
        esum = A.sb("esum", [ROWS, 1])
        lsum = A.sb("lsum", [ROWS, 1])

        ps_a = A.ps("ps_a", [P, 4, P])
        ps_q = A.ps("ps_q", [P, 512])
        ps_k = A.ps("ps_k", [P, 512])
        ps_v = A.ps("ps_v", [P, 512])
        ps_s = [A.ps(f"ps_s{n}", [P, 4, P]) for n in range(2)]
        ps_t = [A.ps(f"ps_t{n}", [P, 4, P]) for n in range(2)]

        w_in, w_ready, wz_ready = A.sem("w_in"), A.sem("w_ready"), A.sem("zero_ready")
        xr_ready, mx_ready, sub_ready = A.sem("xr_ready"), A.sem("mx_ready"), A.sem("sub_ready")
        rec_ready, on_ready, y_ready = A.sem("rec_ready"), A.sem("on_ready"), A.sem("y_ready")
        xrT_ps, q_ps, k_ps, v_ps, s_ps = (A.sem(n) for n in ("xrT_ps", "q_ps", "k_ps", "v_ps", "s_ps"))
        pT_ps, o_ps, oT_ps, f_ps = (A.sem(n) for n in ("pT_ps", "o_ps", "oT_ps", "f_ps"))
        xrT_sb, q_sb, k_sb, v_sb = (A.sem(n) for n in ("xrT_sb", "q_sb", "k_sb", "v_sb"))
        p_sb, pT_sb, oT_sb = (A.sem(n) for n in ("p_sb", "pT_sb", "oT_sb"))
        smax_ready, tmin_ready, esum_ready, lsum_ready, na_ready = (
            A.sem(n) for n in ("smax_ready", "tmin_ready", "esum_ready", "lsum_ready", "na_ready"))
        u_ready, sc_ready = A.sem("u_ready"), A.sem("sc_ready")
        block = ctx.enter_context(nc.Block())

        D0, D1 = 2, 2 + ITERS - 1

        def windows(eng, body):
            for i in range(-1, D0):
                body(i, None)
            with eng.Fori(D0, D1) as i:
                body(i, i - D0)
            with eng.Fori(D1, NT - 2) as i:
                body(i, None)
            for i in range(NT - 2, NT + 2):
                body(i, None)

        def live(i, lag=0):
            return not isinstance(i, int) or 0 <= i - lag < NT

        @block.sync
        def _(sp):
            sp.dma_start(wraw[:, 0], w["wq"]).then_inc(w_in, 16)
            sp.dma_start(wraw[:, 1:3], w["wkv"].rearrange("c (s n) -> c s n", s=2)).then_inc(w_in, 16)
            sp.dma_start(gamma[:], w["gamma"].rearrange("(c o) -> c o", o=1)).then_inc(w_in, 16)
            sp.dma_start(wo[:], w["wo"].rearrange("(p r) c -> r p c", r=P)).then_inc(w_in, 16)

        @block.gpsimd
        def _(pool):
            nc.gpsimd.memset(qz[:], 0.0)
            nc.gpsimd.memset(v[:, :, DH:DH + 1], 1.0).then_inc(wz_ready, 1)

        @block.tensor
        def _(pe):
            pe.wait_ge(w_ready, 1)
            pe.wait_ge(w_in, 64)

            def body(i, d):
                if live(i):
                    pe.wait_ge(xrT_sb, i + 1)
                    if past(i, 1):
                        pe.wait_ge(v_sb, i)
                    nc.tensor.matmul(ps_v[:], xrT[:], wqkv[:, 2, :], start=True, stop=True).then_inc(v_ps, 1)
                    if past(i, 2):
                        pe.wait_ge(on_ready, i - 1)
                    for p in range(PAIRS):
                        last = nc.tensor.matmul(ps_q[:, p * P:(p + 1) * P], wqkv[:, 0, p * P:(p + 1) * P], xrT[:],
                                                start=True, stop=True)
                    last.then_inc(q_ps, 1)
                    for p in range(PAIRS):
                        last = nc.tensor.matmul(ps_k[:, p * P:(p + 1) * P], wqkv[:, 1, p * P:(p + 1) * P], xrT[:],
                                                start=True, stop=True)
                    last.then_inc(k_ps, 1)
                if live(i, 2):
                    pe.wait_ge(on_ready, i - 1)
                    for p in range(PAIRS):
                        last = nc.tensor.transpose(ps_t[1][:, p], on[:, 2 * p:2 * p + 2, :].rearrange("p h d -> p (h d)"), ident[:])
                    last.then_inc(oT_ps, 1)
                if live(i, -1):
                    pe.wait_ge(xr_ready, i + 2)
                    if past(i, 3):
                        pe.wait_ge(y_ready, i - 2)
                    nc.tensor.transpose(ps_a[:, 0], xr[:], ident[:]).then_inc(xrT_ps, 1)
                if live(i):
                    pe.wait_ge(q_sb, i + 1)
                    pe.wait_ge(k_sb, i + 1)
                    if past(i, 1):
                        pe.wait_ge(sub_ready, 2 * i)
                    for n in range(2):
                        for h in range(4 * n, 4 * n + 4):
                            last = nc.tensor.matmul(ps_s[n][:, h % 4], qz[:, h // 2, h % 2, :], kT[:, h // 2, :],
                                                    start=True, stop=True)
                        last.then_inc(s_ps, 1)
                if live(i, 1):
                    pe.wait_ge(p_sb, 2 * i)
                    for n in range(2):
                        if n == 1 and live(i, 2):
                            pe.wait_ge(oT_sb, i - 1)
                        for h in range(4 * n, 4 * n + 4):
                            last = nc.tensor.transpose(ps_t[n][:, h % 4], prob[:, h], ident[:])
                        last.then_inc(pT_ps, 1)
                if live(i, 1):
                    pe.wait_ge(v_sb, i)
                    for n in range(2):
                        pe.wait_ge(pT_sb, 2 * i - 1 + n)
                        bank = (ps_q, ps_k)[n][:, 0:4 * (DH + 1)].rearrange("p (h d) -> p h d", h=4)
                        for h in range(4 * n, 4 * n + 4):
                            last = nc.tensor.matmul(bank[:, h % 4], probT[:, h], v[:, h], start=True, stop=True)
                    last.then_inc(o_ps, 1)
                if live(i, 2):
                    pe.wait_ge(oT_sb, i - 1)
                    if live(i, -1):
                        pe.wait_ge(xrT_sb, i + 2)
                    if past(i, 3):
                        pe.wait_ge(y_ready, i - 2)
                    for p in range(PAIRS):
                        last = nc.tensor.matmul(ps_a[:, 2], oT[:, p], wo[:, p], start=p == 0, stop=p == PAIRS - 1)
                    last.then_inc(f_ps, 1)

            windows(pe, body)

        @block.scalar
        def _(act):
            nc.scalar.preload_act_table_set("natural_log_exp_and_others")
            act.wait_ge(wz_ready, 1)

            def body(i, d):
                if live(i):
                    act.wait_ge(q_ps, i + 1)
                    if past(i, 1):
                        act.wait_ge(s_ps, 2 * i)
                    for s in range(2):
                        last = nc.scalar.copy(qz[64 * s:64 * s + 64, :, s, :],
                                              ps_q[64 * s:64 * s + 64, :].rearrange("p (a b) -> p a b", a=PAIRS))
                    last.then_inc(q_sb, 1)
                    act.wait_ge(k_ps, i + 1)
                    nc.scalar.copy(kT[:], ps_k[:].rearrange("p (a b) -> p a b", a=PAIRS)).then_inc(k_sb, 1)
                if live(i, 2):
                    act.wait_ge(oT_ps, i - 1)
                    if past(i, 3):
                        act.wait_ge(f_ps, i - 2)
                    nc.scalar.copy(oT[:], ps_t[1][:]).then_inc(oT_sb, 1)
                if live(i, -1):
                    act.wait_ge(xrT_ps, i + 2)
                    if past(i, 0):
                        act.wait_ge(k_ps, i + 1)
                    nc.scalar.copy(xrT[:], ps_a[:, 0]).then_inc(xrT_sb, 1)
                if live(i, 1):
                    if past(i, 2):
                        act.wait_ge(o_ps, i - 1)
                    for n in range(2):
                        act.wait_ge(pT_ps, 2 * i - 1 + n)
                        nc.scalar.copy(probT[:, 4 * n:4 * n + 4], ps_t[n][:]).then_inc(pT_sb, 1)
                if live(i):
                    for n in range(2):
                        act.wait_ge(sub_ready, 2 * i + 1 + n)
                        if past(i, 1):
                            act.wait_ge(pT_ps, 2 * i)
                        nc.scalar.activation(prob[:, 4 * n:4 * n + 4], ssub[:, 4 * n:4 * n + 4], ACT.Exp, scale=SM)\
                            .then_inc(p_sb, 1)
                if d is not None:
                    act.wait_ge(tmin_ready, d + 1)
                    nc.scalar.activation(eexp[:], tmin[:], ACT.Exp, bias=nm[:], accum_out=esum[:]).then_inc(esum_ready, 1)
                if live(i):
                    if past(i, 1):
                        act.wait_ge(o_ps, i)
                    act.wait_ge(v_ps, i + 1)
                    nc.scalar.copy(v[:, :, 0:DH], ps_v[:].rearrange("p (h d) -> p h d", h=HEADS)).then_inc(v_sb, 1)
                if d is not None:
                    act.wait_ge(esum_ready, d + 1)
                    nc.scalar.activation(lsum[:], esum[:], ACT.Ln).then_inc(lsum_ready, 1)

            windows(act, body)
            act.wait_ge(u_ready, 1)
            nc.scalar.activation(scores[:], tmin[:], ACT.Exp).then_inc(sc_ready, 1)

        @block.vector
        def _(dve):
            dve.wait_ge(w_in, 64)
            nc.vector.tensor_scalar(wqkv[:], wraw[:], gamma[:, 0:1], None, ALU.mult).then_inc(w_ready, 1)
            nc.vector.tensor_reduce(smax[:], s_rows[:], X_AX, ALU.max).then_inc(smax_ready, 1)
            nc.vector.tensor_scalar(na[:], logk[:], -1.0, float(np.log(T)), ALU.mult, ALU.add).then_inc(na_ready, 1)
            dve.wait_ge(smax_ready, 1)

            def make_xr(j):
                nc.vector.tensor_scalar(xr[:], x[:, bass.ds(j, 1), :].rearrange("p o c -> p (o c)"),
                                        scale_a[:, bass.ds(j, 1)], shift_b[:, bass.ds(j, 1)],
                                        ALU.mult, ALU.add).then_inc(xr_ready, 1)

            make_xr(0)

            def body(i, d):
                if d is not None:
                    dve.wait_ge(na_ready, d + 1)
                    dve.wait_ge(lsum_ready, d)
                    nc.vector.tensor_scalar(nm[:], smax[:], na[:], -1.0, ALU.min, ALU.mult)
                    nc.vector.tensor_scalar(tmin[:], s_rows[:], na[:], None, ALU.min).then_inc(tmin_ready, 1)
                if live(i):
                    for n in range(2):
                        dve.wait_ge(s_ps, 2 * i + 1 + n)
                        nc.vector.tensor_reduce(mx[:, 4 * n:4 * n + 4], ps_s[n][:], X_AX, ALU.max).then_inc(mx_ready, 1)
                    for n in range(2):
                        dve.wait_ge(mx_ready, 2 * i + 1 + n)
                        if past(i, 1):
                            dve.wait_ge(p_sb, 2 * i)
                        nc.vector.tensor_tensor(
                            ssub[:, 4 * n:4 * n + 4], ps_s[n][:],
                            mx[:, 4 * n:4 * n + 4].rearrange("p (h o) -> p h o", o=1).broadcast_to([P, 4, P]),
                            ALU.subtract).then_inc(sub_ready, 1)
                if live(i, -2):
                    dve.wait_ge(xrT_ps, i + 2)
                    make_xr(i + 2)
                if live(i, 1):
                    dve.wait_ge(o_ps, i)
                    banks = [b[:, 0:4 * (DH + 1)].rearrange("p (h d) -> p h d", h=4) for b in (ps_q, ps_k)]
                    for n in range(2):
                        last = nc.vector.reciprocal(rec[:, 4 * n:4 * n + 4].rearrange("p (h o) -> p h o", o=1),
                                                    banks[n][:, :, DH:DH + 1])
                    last.then_inc(rec_ready, 1)
                    dve.wait_ge(rec_ready, i)
                    if past(i, 2):
                        dve.wait_ge(oT_ps, i - 1)
                    for n in range(2):
                        last = nc.vector.tensor_tensor(
                            on[:, 4 * n:4 * n + 4], banks[n][:, :, 0:DH],
                            rec[:, 4 * n:4 * n + 4].rearrange("p (h o) -> p h o", o=1).broadcast_to([P, 4, DH]),
                            ALU.mult)
                    last.then_inc(on_ready, 1)
                if live(i, 2):
                    dve.wait_ge(f_ps, i - 1)
                    j = i - 2
                    nc.vector.scalar_tensor_tensor(
                        y[:, bass.ds(j, 1), :].rearrange("p o c -> p (o c)"), ps_a[:, 2], 0.5,
                        x[:, bass.ds(j, 1), :].rearrange("p o c -> p (o c)"), ALU.mult, ALU.add).then_inc(y_ready, 1)
                if d is not None:
                    dve.wait_ge(lsum_ready, d + 1)
                    nc.vector.tensor_scalar(na[:], lsum[:], nm[:], logk[:], ALU.subtract, ALU.subtract)\
                        .then_inc(na_ready, 1)

            windows(dve, body)
            dve.wait_ge(na_ready, ITERS)
            nc.vector.tensor_scalar(tmin[:], s_rows[:], na[:], 0.0, ALU.subtract, ALU.min).then_inc(u_ready, 1)
            dve.wait_ge(sc_ready, 1)


def route_tokens(nc, tag, scores, posw, ident):
    with ExitStack() as ctx:
        A = Arena(nc, ctx, tag)
        work = A.sb("work", [ROWS, T])
        top = A.sb("top", [ROWS, 8])
        mask = A.sb("mask", [ROWS, T])
        ones = A.sb("ones", [ROWS, T])
        rank = A.sb("rank", [ROWS, T])
        one_minus = A.sb("one_minus", [ROWS, T])
        weight = A.sb("weight", [ROWS, T])
        psT = A.ps("psT", [P, 2, TPB, ROWS])
        step, rows_ready, rows_ps, ones_ready = (A.sem(n) for n in ("step", "rows_ready", "rows_ps", "ones_ready"))
        block = ctx.enter_context(nc.Block())

        @block.gpsimd
        def _(pool):
            nc.gpsimd.memset(ones[:], 1.0).then_inc(ones_ready, 1)

        @block.tensor
        def _(pe):
            pe.wait_ge(rows_ready, 1)
            for k, rows in enumerate((rank, weight)):
                for j in range(TPB):
                    last = nc.tensor.transpose(psT[:, k, j], rows[:, j * P:(j + 1) * P], ident[0:ROWS, 0:ROWS])
            last.then_inc(rows_ps, 1)

        @block.vector
        def _(dve):
            ch = Chain(dve, step)
            ch.step(nc.vector.tensor_copy(work[:], scores[:]))
            for r in range(NKV // 8):
                ch.step(nc.vector.max(top[:], work[:]))
                ch.step(nc.vector.match_replace(work[:], top[:], work[:], -1.0))
                if r == NQ // 8 - 1:
                    ch.step(nc.vector.tensor_scalar(mask[0:KV0, :], work[0:KV0, :], -1.0, None, ALU.is_equal))
            ch.step(nc.vector.tensor_scalar(mask[KV0:ROWS, :], work[KV0:ROWS, :], -1.0, None, ALU.is_equal))
            dve.wait_ge(ones_ready, 1)
            ch.step(nc.vector.tensor_tensor_scan(rank[:], ones[:], mask[:], 0.0, ALU.mult, ALU.add))
            ch.step(nc.vector.tensor_tensor(rank[:], rank[:], mask[:], ALU.mult))
            ch.step(nc.vector.tensor_scalar(rank[:], rank[:], -1.0, None, ALU.add))
            ch.step(nc.vector.tensor_scalar(one_minus[:], scores[:], -1.0, 1.0, ALU.mult, ALU.add))
            nc.vector.tensor_tensor(weight[:], scores[:], one_minus[:], ALU.add).then_inc(rows_ready, 1)
            dve.wait_ge(rows_ps, 1)
            ch.step(nc.vector.tensor_copy(posw[:], psT[:]))


def heavy_attention(nc, tag, x, y, scale_a, shift_b, posw, w, ident, iota):
    SM = DH ** -0.5
    NS = NQ + NKV
    HH = HEADS // 2
    with ExitStack() as ctx:
        A = Arena(nc, ctx, tag)
        wraw = A.sb("wraw", [P, 3 * HID])
        gamma = A.sb("gamma", [P, 1])
        wq = A.sb("wq", [P, HID])
        wk = A.sb("wk", [P, HID])
        wv = A.sb("wv", [P, HID])
        wo = A.sb("wo", [P, PAIRS, C])
        pcol = A.sb("pcol", [P, 2, TPB, 2])
        wcol = A.sb("wcol", [P, 2, TPB])
        xr = A.sb("xr", [P, TPB, C])
        sel = A.sb("sel", [P, TPB, NS])
        wsel = A.sb("wsel", [P, TPB, NQ])
        gate = A.sb("gate", [P, 2])
        xsT = A.sb("xsT", [P, NS])
        vsc = A.sb("vsc", [P, 2])
        qz = A.sb("qz", [P, PAIRS, 2, P])
        kT = A.sb("kT", [P, PAIRS, NKV])
        v = A.sb("v", [P, 2, HEADS, DH + 1])
        mx = A.sb("mx", [P, HEADS])
        ssub = A.sb("ssub", [P, HEADS, NKV])
        prob = A.sb("prob", [P, HEADS, NKV])
        probT = A.sb("probT", [P, HEADS, 2, P])
        rec = A.sb("rec", [P, HEADS])
        on = A.sb("on", [P, HEADS, DH])
        oT = A.sb("oT", [P, PAIRS, P])
        wT = A.sb("wT", [P, TPB, P])
        routed = A.sb("routed", [P, C])

        ps_s = [A.ps(f"ps_s{n}", [P, HH, NKV]) for n in range(2)]
        ps4 = A.ps("ps4", [P, 512])
        ps5 = A.ps("ps5", [P, 512])
        ps6 = A.ps("ps6", [P, 512])
        ps7 = A.ps("ps7", [P, 512])

        S = {n: A.sem(n) for n in (
            "w_in", "w_ready", "zeroed", "pcol_ready", "wcol_ready", "sel_ready", "wsel_ready", "xr_ready",
            "g_ps", "q_ps", "k_ps", "v_ps", "s_ps", "pT_ps", "o_ps", "oT_ps", "wT_ps", "f_ps", "sc_ps",
            "xs_sb", "q_sb", "k_sb", "v_sb", "p_sb", "pT_sb", "oT_sb", "wT_sb", "f_sb",
            "mx_ready", "sub_ready", "rec_ready", "on_ready", "y_ready", "xr_step")}
        block = ctx.enter_context(nc.Block())

        def batches(eng, body):
            for i in range(-1, 2):
                body(i)
            with eng.Fori(2, B - 2) as i:
                body(i)
            for i in range(B - 2, B + 1):
                body(i)

        def live(i, lag=0):
            return not isinstance(i, int) or 0 <= i - lag < B

        @block.sync
        def _(sp):
            sp.dma_start(wraw[:, 0:HID], w["wq"]).then_inc(S["w_in"], 16)
            sp.dma_start(wraw[:, HID:3 * HID], w["wkvT"]).then_inc(S["w_in"], 16)
            sp.dma_start(gamma[:], w["gamma"].rearrange("(c o) -> c o", o=1)).then_inc(S["w_in"], 16)
            sp.dma_start(wo[:], w["wo"].rearrange("(p r) c -> r p c", r=P)).then_inc(S["w_in"], 16)

        @block.gpsimd
        def _(pool):
            nc.gpsimd.memset(qz[:], 0.0)
            nc.gpsimd.memset(v[:, :, :, DH:DH + 1], 1.0).then_inc(S["zeroed"], 1)

            def body(i):
                if live(i, -1):
                    pool.wait_ge(S["pcol_ready"], i + 2)
                    if past(i, 0):
                        pool.wait_ge(S["g_ps"], i + 1)
                    nc.gpsimd.tensor_tensor(gate[:, 0:1], iota[:, 0:1], pcol[:, 0, 0, 0:1], ALU.add)
                    for j in range(TPB):
                        nc.gpsimd.tensor_scalar(sel[:, j, 0:NQ], iota[:, 0:NQ], pcol[:, 0, j, 0:1], None, ALU.is_equal)
                        last = nc.gpsimd.tensor_scalar(sel[:, j, NQ:NS], iota[:], pcol[:, 0, j, 1:2], None, ALU.is_equal)
                    last.then_inc(S["sel_ready"], 1)
                if live(i):
                    pool.wait_ge(S["wcol_ready"], i + 1)
                    if past(i, 1):
                        pool.wait_ge(S["wT_ps"], i)
                    nc.gpsimd.tensor_tensor(gate[:, 1:2], iota[:, 0:1], wcol[:, 0, 0:1], ALU.add)
                    for j in range(TPB):
                        last = nc.gpsimd.tensor_scalar(wsel[:, j], iota[:, 0:NQ], wcol[:, 0, j:j + 1], wcol[:, 1, j:j + 1],
                                                       ALU.is_equal, ALU.mult)
                    last.then_inc(S["wsel_ready"], 1)

            batches(pool, body)

        @block.tensor
        def _(pe):
            pe.wait_ge(S["w_ready"], 1)
            pe.wait_ge(S["w_in"], 64)

            def body(i):
                if live(i):
                    pe.wait_ge(S["q_sb"], i + 1)
                    pe.wait_ge(S["k_sb"], 2 * i + 2)
                    for n in range(2):
                        if past(i, 1):
                            pe.wait_ge(S["pT_sb"], 4 * i - 2 + 2 * n)
                        for h in range(HH * n, HH * n + HH):
                            last = nc.tensor.matmul(ps_s[n][:, h % HH], qz[:, h // 2, h % 2, :], kT[:, h // 2, :],
                                                    start=True, stop=True)
                        last.then_inc(S["s_ps"], 1)
                if live(i, 1):
                    pe.wait_ge(S["on_ready"], i)
                    if live(i):
                        pe.wait_ge(S["v_sb"], 2 * i + 1)
                    for p in range(PAIRS):
                        last = nc.tensor.transpose(ps4[:, p * P:(p + 1) * P],
                                                   on[:, 2 * p:2 * p + 2, :].rearrange("p h d -> p (h d)"), ident[:])
                    last.then_inc(S["oT_ps"], 1)
                    pe.wait_ge(S["wsel_ready"], i)
                    for j in range(TPB):
                        last = nc.tensor.transpose(ps6[:, j * P:(j + 1) * P], wsel[:, j], ident[:])
                    last.then_inc(S["wT_ps"], 1)
                    pe.wait_ge(S["oT_sb"], i)
                    for p in range(PAIRS):
                        last = nc.tensor.matmul(ps5[:, 0:C], oT[:, p], wo[:, p], start=p == 0, stop=p == PAIRS - 1)
                    last.then_inc(S["f_ps"], 1)
                if live(i, -1):
                    pe.wait_ge(S["sel_ready"], i + 2)
                    pe.wait_ge(S["xr_ready"], i + 2)
                    if past(i, 0) and not live(i, 1):
                        pe.wait_ge(S["v_sb"], 2 * i + 2)
                    for j in range(TPB):
                        nc.tensor.matmul(ps4[:, 0:NS], xr[:, j], sel[:, j], start=j == 0, stop=j == TPB - 1)
                    for c in range(2):
                        for j in range(TPB):
                            last = nc.tensor.matmul(ps4[:, NS + c:NS + c + 1], sel[:, j, NQ + c * P:NQ + (c + 1) * P],
                                                    pcol[:, 1, j, 1:2], start=j == 0, stop=j == TPB - 1)
                    last.then_inc(S["g_ps"], 1)
                if live(i, 1):
                    pe.wait_ge(S["f_sb"], i)
                    pe.wait_ge(S["wT_sb"], i)
                    for j in range(TPB):
                        last = nc.tensor.matmul(ps7[:, j * P:(j + 1) * P], wT[:, j], routed[:], start=True, stop=True)
                    last.then_inc(S["sc_ps"], 1)
                if live(i):
                    pe.wait_ge(S["p_sb"], 2 * i + 1)
                    for h in range(HH):
                        for c in range(2):
                            last = nc.tensor.transpose(ps_s[0][:, h, c * P:(c + 1) * P], prob[:, h, c * P:(c + 1) * P], ident[:])
                    last.then_inc(S["pT_ps"], 1)
                if live(i, -1):
                    pe.wait_ge(S["xs_sb"], i + 2)
                    for p in range(PAIRS):
                        last = nc.tensor.matmul(ps5[:, p * P:(p + 1) * P], wq[:, p * P:(p + 1) * P], xsT[:, 0:NQ],
                                                start=True, stop=True)
                    last.then_inc(S["q_ps"], 1)
                    for n, bank in enumerate((ps6, ps7)):
                        if n and live(i, 1):
                            pe.wait_ge(S["y_ready"], i)
                        for p in range(2):
                            pr = 2 * n + p
                            last = nc.tensor.matmul(bank[:, p * NKV:(p + 1) * NKV], wk[:, pr * P:(pr + 1) * P], xsT[:, NQ:NS],
                                                    start=True, stop=True)
                        last.then_inc(S["k_ps"], 1)
                if live(i):
                    pe.wait_ge(S["p_sb"], 2 * i + 2)
                    for h in range(HH):
                        for c in range(2):
                            last = nc.tensor.transpose(ps_s[1][:, h, c * P:(c + 1) * P], prob[:, HH + h, c * P:(c + 1) * P], ident[:])
                    last.then_inc(S["pT_ps"], 1)
                if live(i, -1):
                    for c, bank in enumerate((ps4, ps5)):
                        if c:
                            pe.wait_ge(S["q_sb"], i + 2)
                        nc.tensor.matmul(bank[:], xsT[:, NQ + c * P:NQ + (c + 1) * P], wv[:], start=True, stop=True)\
                            .then_inc(S["v_ps"], 1)
                if live(i):
                    if live(i, -1):
                        pe.wait_ge(S["k_sb"], 2 * i + 4)
                    pe.wait_ge(S["v_sb"], 2 * i + 2)
                    for n, bank in enumerate((ps6, ps7)):
                        pe.wait_ge(S["pT_sb"], 4 * i + 2 * n + 2)
                        if n and live(i, 1) and not live(i, -1):
                            pe.wait_ge(S["y_ready"], i)
                        for h in range(HH):
                            for c in range(2):
                                last = nc.tensor.matmul(bank[:, h * (DH + 1):(h + 1) * (DH + 1)], probT[:, HH * n + h, c],
                                                        v[:, c, HH * n + h], start=c == 0, stop=c == 1)
                        last.then_inc(S["o_ps"], 1)

            batches(pe, body)

        @block.scalar
        def _(act):
            act.wait_ge(S["zeroed"], 1)

            def body(i):
                if live(i):
                    if past(i, 1):
                        act.wait_ge(S["o_ps"], 2 * i)
                    for c, bank in enumerate((ps4, ps5)):
                        act.wait_ge(S["v_ps"], 2 * i + 1 + c)
                        nc.scalar.activation(v[:, c, :, 0:DH], bank[:].rearrange("p (h d) -> p h d", h=HEADS), ACT.Copy,
                                             scale=vsc[:, c:c + 1]).then_inc(S["v_sb"], 1)
                if live(i, 1):
                    act.wait_ge(S["oT_ps"], i)
                    nc.scalar.copy(oT[:], ps4[:].rearrange("p (a b) -> p a b", a=PAIRS)).then_inc(S["oT_sb"], 1)
                    act.wait_ge(S["wT_ps"], i)
                    nc.scalar.copy(wT[:], ps6[:].rearrange("p (a b) -> p a b", a=TPB)).then_inc(S["wT_sb"], 1)
                    act.wait_ge(S["f_ps"], i)
                    if past(i, 2):
                        act.wait_ge(S["sc_ps"], i - 1)
                    nc.scalar.copy(routed[:], ps5[:, 0:C]).then_inc(S["f_sb"], 1)
                if live(i):
                    act.wait_ge(S["sub_ready"], 2 * i + 1)
                    nc.scalar.activation(prob[:, 0:HH], ssub[:, 0:HH], ACT.Exp, scale=SM).then_inc(S["p_sb"], 1)
                if live(i, -1):
                    act.wait_ge(S["g_ps"], i + 2)
                    nc.scalar.copy(vsc[:], ps4[:, NS:NS + 2])
                    nc.scalar.copy(xsT[:], ps4[:, 0:NS]).then_inc(S["xs_sb"], 1)
                if live(i):
                    act.wait_ge(S["sub_ready"], 2 * i + 2)
                    nc.scalar.activation(prob[:, HH:HEADS], ssub[:, HH:HEADS], ACT.Exp, scale=SM).then_inc(S["p_sb"], 1)
                    act.wait_ge(S["pT_ps"], 2 * i + 1)
                    if past(i, 1):
                        act.wait_ge(S["o_ps"], 2 * i)
                    for n in range(2):
                        nc.scalar.copy(probT[:, 2 * n:2 * n + 2],
                                       ps_s[0][:, 2 * n:2 * n + 2].rearrange("p h (c q) -> p h c q", c=2)).then_inc(S["pT_sb"], 1)
                if live(i, -1):
                    act.wait_ge(S["q_ps"], i + 2)
                    for s in range(2):
                        last = nc.scalar.copy(qz[64 * s:64 * s + 64, :, s, :],
                                              ps5[64 * s:64 * s + 64, :].rearrange("p (a b) -> p a b", a=PAIRS))
                    last.then_inc(S["q_sb"], 1)
                    for n, bank in enumerate((ps6, ps7)):
                        act.wait_ge(S["k_ps"], 2 * i + 3 + n)
                        nc.scalar.copy(kT[:, 2 * n:2 * n + 2], bank[:].rearrange("p (a b) -> p a b", a=2)).then_inc(S["k_sb"], 1)
                if live(i):
                    act.wait_ge(S["pT_ps"], 2 * i + 2)
                    for n in range(2):
                        nc.scalar.copy(probT[:, HH + 2 * n:HH + 2 * n + 2],
                                       ps_s[1][:, 2 * n:2 * n + 2].rearrange("p h (c q) -> p h c q", c=2)).then_inc(S["pT_sb"], 1)

            batches(act, body)

        @block.vector
        def _(dve):
            dve.wait_ge(S["w_in"], 64)
            kv = wraw[:, HID:3 * HID].rearrange("p (h s d) -> p s h d", h=HEADS, s=2)
            nc.vector.tensor_scalar(wq[:], wraw[:, 0:HID], gamma[:, 0:1], None, ALU.mult)
            nc.vector.tensor_scalar(wk[:].rearrange("p (h d) -> p h d", h=HEADS), kv[:, 0], gamma[:, 0:1], None, ALU.mult)
            nc.vector.tensor_scalar(wv[:].rearrange("p (h d) -> p h d", h=HEADS), kv[:, 1], gamma[:, 0:1], None, ALU.mult)\
                .then_inc(S["w_ready"], 1)

            def prepare(b):
                for s in range(2):
                    last = nc.vector.tensor_copy(pcol[:, :, :, s:s + 1], posw[:, :, :, bass.ds(KV0 * s + b, 1)])
                last.then_inc(S["pcol_ready"], 1)
                nc.vector.tensor_tensor(xr[:], x[:, bass.ds(TPB * b, TPB), :],
                                        scale_a[:, bass.ds(TPB * b, TPB)].rearrange("p (n o) -> p n o", o=1).broadcast_to([P, TPB, C]),
                                        ALU.mult).then_inc(S["xr_step"], 1)
                dve.wait_ge(S["xr_step"], b + 1)
                nc.vector.tensor_tensor(xr[:], xr[:],
                                        shift_b[:, bass.ds(TPB * b, TPB)].rearrange("p (n o) -> p n o", o=1).broadcast_to([P, TPB, C]),
                                        ALU.add).then_inc(S["xr_ready"], 1)

            def columns(b):
                nc.vector.tensor_copy(wcol[:].rearrange("p a (j o) -> p a j o", o=1),
                                      posw[:, :, :, bass.ds(b, 1)]).then_inc(S["wcol_ready"], 1)

            prepare(0)
            columns(0)

            def body(i):
                if live(i):
                    for n in range(2):
                        dve.wait_ge(S["s_ps"], 2 * i + 1 + n)
                        nc.vector.tensor_reduce(mx[:, HH * n:HH * n + HH], ps_s[n][:], X_AX, ALU.max).then_inc(S["mx_ready"], 1)
                        dve.wait_ge(S["mx_ready"], 2 * i + 1 + n)
                        if past(i, 1):
                            dve.wait_ge(S["p_sb"], 2 * i)
                        nc.vector.tensor_tensor(
                            ssub[:, HH * n:HH * n + HH], ps_s[n][:],
                            mx[:, HH * n:HH * n + HH].rearrange("p (h o) -> p h o", o=1).broadcast_to([P, HH, NKV]),
                            ALU.subtract).then_inc(S["sub_ready"], 1)
                if live(i, 1):
                    dve.wait_ge(S["sc_ps"], i)
                    ys = y[:, bass.ds(TPB * (i - 1), TPB), :]
                    nc.vector.scalar_tensor_tensor(ys, ps7[:].rearrange("p (a b) -> p a b", a=TPB), 0.5, ys,
                                                   ALU.mult, ALU.add).then_inc(S["y_ready"], 1)
                if live(i, -2):
                    dve.wait_ge(S["g_ps"], i + 2)
                    dve.wait_ge(S["sel_ready"], i + 2)
                    prepare(i + 2)
                if live(i, -1) and past(i, 0):
                    dve.wait_ge(S["wsel_ready"], i + 1)
                    columns(i + 1)
                if live(i):
                    dve.wait_ge(S["o_ps"], 2 * i + 2)
                    banks = [b[:, 0:HH * (DH + 1)].rearrange("p (h d) -> p h d", h=HH) for b in (ps6, ps7)]
                    for n in range(2):
                        last = nc.vector.reciprocal(rec[:, HH * n:HH * n + HH].rearrange("p (h o) -> p h o", o=1),
                                                    banks[n][:, :, DH:DH + 1])
                    last.then_inc(S["rec_ready"], 1)
                    dve.wait_ge(S["rec_ready"], i + 1)
                    if past(i, 1):
                        dve.wait_ge(S["oT_ps"], i)
                    for n in range(2):
                        last = nc.vector.tensor_tensor(
                            on[:, HH * n:HH * n + HH], banks[n][:, :, 0:DH],
                            rec[:, HH * n:HH * n + HH].rearrange("p (h o) -> p h o", o=1).broadcast_to([P, HH, DH]),
                            ALU.mult)
                    last.then_inc(S["on_ready"], 1)

            batches(dve, body)


def norm_stats(nc, tag, x, scale_a, shift_b, beside=None):
    RUN = 8
    with ExitStack() as ctx:
        A = Arena(nc, ctx, tag)
        st = A.sb("st", [P, NT, 6])
        total = A.sb("total", [P, NT])
        diff = A.sb("diff", [P, NT])
        var = A.sb("var", [P, NT])
        stats_ready, step, var_ready, std_ready = (A.sem(n) for n in ("stats_ready", "step", "var_ready", "std_ready"))
        block = ctx.enter_context(nc.Block())
        if beside:
            beside(block)

        @block.scalar
        def _(act):
            act.wait_ge(var_ready, 1)
            nc.scalar.activation(diff[:], var[:], ACT.Sqrt).then_inc(std_ready, 1)

        @block.vector
        def _(dve):
            ch = Chain(dve, step)
            with dve.Fori(0, NT // RUN) as k:
                for j in range(RUN):
                    last = nc.vector.bn_stats(st[:, bass.ds(RUN * k + j, 1), :].rearrange("p o s -> p (o s)"),
                                              x[:, bass.ds(RUN * k + j, 1), :].rearrange("p o c -> p (o c)"))
                last.then_inc(stats_ready, 1)
            dve.wait_ge(stats_ready, NT // RUN)
            col = lambda n: st[:, :, n:n + 1].rearrange("p n o -> p (n o)")
            nc.vector.tensor_tensor(total[:], col(1), col(4), ALU.add)
            nc.vector.tensor_tensor(var[:], col(2), col(5), ALU.add)
            ch.step(nc.vector.tensor_tensor(diff[:], col(1), col(4), ALU.subtract))
            ch.step(nc.vector.tensor_tensor(diff[:], diff[:], diff[:], ALU.mult))
            ch.step(nc.vector.scalar_tensor_tensor(var[:], diff[:], C / 4.0, var[:], ALU.mult, ALU.add))
            nc.vector.tensor_scalar(var[:], var[:], 1.0 / C, LN_EPS, ALU.mult, ALU.add).then_inc(var_ready, 1)
            dve.wait_ge(std_ready, 1)
            ch.step(nc.vector.reciprocal(scale_a[:], diff[:]))
            ch.step(nc.vector.scalar_tensor_tensor(shift_b[:], total[:], -0.5, scale_a[:], ALU.mult, ALU.mult))


LOGIT_MAX = float(np.log(1.0 / 0.01))
AH, AL, AD = 16, 64, 8
RUNS_Q = ((0, 3, 0, True), (3, 2, 1, True), (5, 1, 2, True))
RUNS_K = ((0, 3, 0, False), (3, 2, 0, False), (5, 1, 0, False))
MROW = 96
KROWS = MROW + 3
VPAD = 32
GROUPS = 2
GH = AH // GROUPS


def stacked_attention(nc, tag, latent, y, scale_a, shift_b, w, scratch, ident, identb):
    SM = AD ** -0.5 if latent else 1.0
    UP = 5 if latent else 2
    UB = UP * AH // 2
    UQ = 2 * UP
    nc.disable_value_cache = True
    with ExitStack() as ctx:
        A = Arena(nc, ctx, tag)
        if latent:
            wdT = A.sb("wdT", [P, 3, AH // 2, C])
            wup = A.sb("wup", [P, 3, AD])
            up2 = A.sb("up2", [P, 5, 2, AD])
            cos = A.sb("cos", [P, T])
            sin = A.sb("sin", [P, T])
            maskq = A.sb("maskq", [P, P], BF16)
            maskk = A.sb("maskk", [P, P], BF16)
        else:
            bqk = A.sb("bqk", [P, 2])
            bv = A.sb("bv", [P, 1, C])
            bo = A.sb("bo", [P, 1, C])
            lsc = A.sb("lsc", [P, 2])
            ln = A.sb("ln", [P, T])
            hsc = A.sb("hsc", [P, 1])
            ones8 = A.sb("ones8", [P, P])
            qb = A.sb("qb", [P, T])
            sq = A.sb("sq", [P, T])
            added = A.sb("added", [P, TPB, C])
        weff = A.sb("weff", [P, 5, C])
        wc = A.sb("wc", [P, C])
        xn = A.sb("xn", [P, TPB, C])
        xnT = [A.sb(f"xnT{u}", [P, T]) for u in range(2)]
        t1 = A.sb("t1", [P, T])
        t2 = A.sb("t2", [P, T])
        rr = A.sb("rr", [P, T])
        r1 = A.sb("r1", [P, T])
        parts = A.sb("parts", [P, 2, 3, T], BF16)
        qs = [A.sb(f"qs{u}", [KROWS, AH, T], BF16) for u in range(2)]
        ks = [A.sb(f"ks{u}", [KROWS, AH, T], BF16) for u in range(2)]
        v = [A.sb(f"v{u}", [P, TPB, AH, VPAD]) for u in range(2)]
        mx = A.sb("mx", [P, GROUPS, GH, TPB])
        mres = A.sb("mres", [P, GH * TPB])
        mparts = A.sb("mparts", [P, 3, GH * TPB], BF16)
        mT = A.sb("mT", [3 * GH * TPB, P], BF16)
        prob = [A.sb(f"prob{n}", [P, UQ, T]) for n in range(2)]
        oT = A.sb("oT", [P, T])
        rec = A.sb("rec", [P, TPB, 4])
        yt = A.sb("yt", [P, TPB, AH, AD])
        yT = A.sb("yT", [P, T])

        ps1 = [A.ps(f"ps1_{n}", [P, 512]) for n in range(2)]
        ps2 = [A.ps(f"ps2_{n}", [P, 512]) for n in range(2)]
        ps_o = A.ps("ps_o", [P, 512])
        ps_a = A.ps("ps_a", [P, 512])
        ps_b = A.ps("ps_b", [P, 512])
        ps_c = A.ps("ps_c", [P, 512])
        ps_ab = ps_a[:].bitcast(BF16)

        S = {n: A.sem(n) for n in (
            "w_in", "zeroed", "wrot_ready", "weff_ps", "weff_ready", "setup",
            "xn_step", "xn_ready", "xnT_ps", "xnT_sb", "q_ps", "rope_t", "roped", "r1_step",
            "part_ready", "store_done", "load0", "load1", "s1_ps", "s1_used", "s2_ps", "p_sb", "pv_ps", "o_sb", "otr_ps",
            "rec_ready", "yt_ready", "yT_ps", "yT_sb", "out_ps", "out_done", "v_ps", "v_sb", "m_step", "m_ready",
            "mT_ps", "mT_sb", "mrow0", "mrow1", "qb_ready", "sum_ps", "floored", "ln_ready", "ls_ready", "sum_step")}
        load = (S["load0"], S["load1"])
        mrow = (S["mrow0"], S["mrow1"])

        def prepare(block):
            @block.sync
            def _(sp):
                if latent:
                    for n, key in enumerate(("qdT", "kdT", "vdT")):
                        sp.dma_start(wdT[:, n], w[key].rearrange("(a r) c -> r a c", r=P)).then_inc(S["w_in"], 16)
                    for s in range(2):
                        half = wup[64 * s:64 * s + 64]
                        for n, (k0, k1) in enumerate((("qc", "qe"), ("kc", "ke"))):
                            sp.dma_start(half[:, n, 0:4], w[k0]).then_inc(S["w_in"], 16)
                            sp.dma_start(half[:, n, 4:8], w[k1]).then_inc(S["w_in"], 16)
                        sp.dma_start(half[:, 2, :], w["vu"]).then_inc(S["w_in"], 16)
                    sp.dma_start(wc[:], w["wc"]).then_inc(S["w_in"], 16)
                    sp.dma_start(cos[:], w["cos"]).then_inc(S["w_in"], 16)
                    sp.dma_start(sin[:], w["sin"]).then_inc(S["w_in"], 16)
                    sp.dma_start(maskq[:], w["maskq"]).then_inc(S["w_in"], 16)
                    sp.dma_start(maskk[:], w["maskk"]).then_inc(S["w_in"], 16)
                else:
                    sp.dma_start(weff[:, 0:3], w["winT"].rearrange("c (n m) -> c n m", n=3)).then_inc(S["w_in"], 16)
                    sp.dma_start(wc[:], w["woT"]).then_inc(S["w_in"], 16)
                    for t in range(2):
                        sp.dma_start(bqk[:, t:t + 1], w["bin"][t * C:(t + 1) * C].rearrange("(p o) -> p o", o=1)).then_inc(S["w_in"], 16)
                    sp.dma_start(bv[:], w["bin"][2 * C:3 * C].rearrange("(a b c) -> a b c", a=1, b=1).broadcast_to([P, 1, C])).then_inc(S["w_in"], 16)
                    sp.dma_start(bo[:], w["bo"].rearrange("(a b c) -> a b c", a=1, b=1).broadcast_to([P, 1, C])).then_inc(S["w_in"], 16)
                    sp.dma_start(lsc[:, 1:2], w["ls"].rearrange("(p o) -> p o", o=1)).then_inc(S["w_in"], 16)
                    sp.dma_start(hsc[:], w["hs"].rearrange("(p o) -> p o", o=1)).then_inc(S["w_in"], 16)
                    sp.dma_start(ones8[:], w["ones8"]).then_inc(S["w_in"], 16)
                sp.wait_ge(S["zeroed"], 1)
                if not latent:
                    for u in range(2):
                        for t, stack in enumerate((qs[u], ks[u])):
                            sp.dma_start(stack[6 * AD:6 * AD + 8, :, :], w["block_rows"][t:t + 1].rearrange("a r t -> r a t")
                                         .broadcast_to([8, AH, T])).then_inc(S["w_in"], 16)

            @block.gpsimd
            def _(pool):
                for u in range(2):
                    nc.gpsimd.memset(qs[u][0:MROW], 0.0)
                    nc.gpsimd.memset(ks[u][:], -1.0)
                    nc.gpsimd.memset(v[u][:], 0.0).then_inc(S["setup"], 1)
                pool.wait_ge(S["setup"], 2)
                for u in range(2):
                    last = nc.gpsimd.memset(v[u][:, :, :, AD:AD + 1], 1.0)
                last.then_inc(S["zeroed"], 1)
        norm_stats(nc, tag + "n", y, scale_a, shift_b, beside=prepare)
        block = ctx.enter_context(nc.Block())

        def batches(eng, body):
            for i in range(-3, 2):
                body(i, i % 2)
            with eng.Fori(1, B // 2 - 2) as k:
                for u in range(2):
                    body(2 * k + u, u)
            for i in range(B - 4, B + 1):
                body(i, i % 2)

        def live(i, lag=0):
            return not isinstance(i, int) or 0 <= i - lag < B

        @block.sync
        def _(sp):
            def body(i, u):
                if live(i):
                    m_rows(i, u, 1)
                if live(i, -2):
                    for t in range(2):
                        sp.wait_ge(S["part_ready"], 2 * (i + 2) + 1 + t)
                        if t == 0 and past(i, -1):
                            for g in range(GROUPS):
                                sp.wait_ge(load[g], 96 * (i + 2))
                        for s in range(3):
                            sp.dma_start(scratch[t, s].rearrange("d h t -> h d t"), parts[:, t, s]).then_inc(S["store_done"], 16)
                if live(i, -1):
                    m_rows(i + 1, 1 - u, 0)
                if live(i, -2):
                    sp.wait_ge(S["store_done"], 96 * (i + 3))
                    for g in range(GROUPS):
                        if past(i, 0):
                            sp.wait_ge(S["s2_ps"], UB * i + UB // 2 * (g + 1))
                        heads = slice(GH * g, GH * g + GH)
                        for t, (stack, runs) in enumerate(((qs[u], RUNS_Q), (ks[u], RUNS_K))):
                            for blk, blks, part, stays in runs:
                                if stays:
                                    src = scratch[t, part:part + 1, :, heads, :].rearrange("s d h t -> s d (h t)")\
                                        .broadcast_to([blks, AD, GH * T])
                                else:
                                    src = scratch[t, part:part + blks, :, heads, :].rearrange("s d h t -> (s d) (h t)")
                                sp.dma_start(stack[AD * blk:AD * (blk + blks), heads, :], src).then_inc(load[g], 16)

            def m_rows(b, u, g):
                sp.wait_ge(S["mT_sb"], 2 * b + 1 + g)
                for s in range(3):
                    n = GH * TPB
                    sp.dma_start(qs[u][MROW + s:MROW + s + 1, GH * g:GH * g + GH, :].rearrange("p h (j t) -> p (h j) t", j=TPB),
                                 mT[n * s:n * s + n, :]).then_inc(mrow[g], 16)

            batches(sp, body)

        @block.gpsimd
        def _(pool):
            src, op = ((t1, t2), ALU.add) if latent else ((qb, t1), ALU.mult)

            def body(i, u):
                if live(i, -3):
                    for t in range(2):
                        n = 2 * (i + 3) + t
                        pool.wait_ge(S["rope_t"], n + 1)
                        nc.gpsimd.tensor_tensor(rr[:], src[0][:], src[1][:], op)
                        if past(i, -2):
                            pool.wait_ge(S["store_done"], 96 * (i + 3))
                        nc.gpsimd.tensor_tensor(parts[:, t, 0], src[0][:], src[1][:], op).then_inc(S["roped"], 1)
                        pool.wait_ge(S["roped"], n + 1)
                        nc.gpsimd.tensor_tensor(r1[:], rr[:], parts[:, t, 0], ALU.subtract)
                        nc.gpsimd.tensor_tensor(parts[:, t, 1], rr[:], parts[:, t, 0], ALU.subtract).then_inc(S["r1_step"], 1)
                        pool.wait_ge(S["r1_step"], n + 1)
                        nc.gpsimd.tensor_tensor(parts[:, t, 2], r1[:], parts[:, t, 1], ALU.subtract).then_inc(S["part_ready"], 1)

            batches(pool, body)

        def units(pair):
            h = 2 * pair
            if not latent:
                return [[(P * j, P, h + k, j) for j in range(TPB)] for k in range(2)]
            return [[(0, 512, h, 0)], [(0, 384, h, 1), (384, 128, h, 3)],
                    [(0, 512, h + 1, 0)], [(0, 384, h + 1, 1), (384, 128, h + 1, 3)],
                    [(0, 256, h, 2), (256, 256, h + 1, 2)]]

        @block.tensor
        def _(pe):
            if latent:
                pe.wait_ge(S["w_in"], 18 * 16)
                pe.wait_ge(S["wrot_ready"], 2)
                for n in range(5):
                    bank = (ps_a, ps_b)[n // 4]
                    for p in range(AH // 2):
                        col = (n % 4) * C + 2 * AD * p
                        last = nc.tensor.matmul(bank[:, col:col + 2 * AD], wdT[:, n % 3, p, :],
                                                up2[:, n].rearrange("p s d -> p (s d)"), start=True, stop=True)
                last.then_inc(S["weff_ps"], 1)
            else:
                pe.wait_ge(S["w_in"], 13 * 16)
            pe.wait_ge(S["weff_ready"], 1)
            pe.wait_ge(S["zeroed"], 1)

            def s1_unit(b, u, n, pair, k):
                if past(n, 2):
                    pe.wait_ge(S["s1_used"], n - 1)
                bank = ps1[(UP * pair + k) % 2]
                for (col, width, h, blk) in units(pair)[k]:
                    if not latent:
                        at = slice(blk * P, (blk + 1) * P)
                        last = nc.tensor.matmul(bank[:, col:col + P], qs[u][0:MROW, h, at], ks[u][0:MROW, h, at],
                                                start=True, stop=True)
                        continue
                    qblk = TPB - 1 - blk
                    last = nc.tensor.matmul(bank[:, col:col + width], qs[u][0:MROW, h, qblk * P:(qblk + 1) * P],
                                            ks[u][0:MROW, h, 0:width], start=True, stop=False)
                    last = nc.tensor.matmul(bank[:, col + width - P:col + width], identb[:], maskq[:], start=False, stop=True)
                last.then_inc(S["s1_ps"], 1)

            def s2_unit(b, u, n, pair, k):
                if past(n, 2):
                    pe.wait_ge(S["p_sb"], n - 1)
                bank = ps2[(UP * pair + k) % 2]
                for (col, width, h, blk) in units(pair)[k]:
                    if not latent:
                        at = slice(blk * P, (blk + 1) * P)
                        last = nc.tensor.matmul(bank[:, col:col + P], ks[u][:, h, at], qs[u][:, h, at], start=True, stop=True)
                        continue
                    last = nc.tensor.matmul(bank[:, col:col + width], ks[u][:, h, blk * P:(blk + 1) * P],
                                            qs[u][:, h, blk * P:T], start=True, stop=False)
                    last = nc.tensor.matmul(bank[:, col:col + P], identb[:], maskk[:], start=False, stop=True)
                last.then_inc(S["s2_ps"], 1)

            def pv(b, u, q):
                pe.wait_ge(S["p_sb"], UB * b + UQ * (q + 1))
                pe.wait_ge(S["v_sb"], b + 1)
                if past(4 * b + q, 1):
                    pe.wait_ge(S["o_sb"], 4 * b + q)
                for blk in range(TPB):
                    for j in range(4):
                        if not latent:
                            at = slice(blk * P, (blk + 1) * P)
                            last = nc.tensor.matmul(ps_o[32 * j:32 * j + 32, at], v[u][:, blk, 4 * q + j, :],
                                                    prob[q % 2][:, j, at], start=True, stop=True)
                            continue
                        unit, col = {0: (5 * (j // 2) + 2 * (j % 2), 0), 1: (5 * (j // 2) + 2 * (j % 2) + 1, 0),
                                     2: (5 * (j // 2) + 4, 256 * (j % 2)), 3: (5 * (j // 2) + 2 * (j % 2) + 1, 384)}[blk]
                        width = T - blk * P
                        last = nc.tensor.matmul(ps_o[32 * j:32 * j + 32, blk * P:T], v[u][:, blk, 4 * q + j, :],
                                                prob[q % 2][:, unit, col:col + width], start=blk == 0, stop=blk == TPB - 1)
                last.then_inc(S["pv_ps"], 1)

            def otr(b, q):
                pe.wait_ge(S["o_sb"], 4 * b + q + 1)
                wait_a(b, "otr", q)
                for j in range(TPB):
                    last = nc.tensor.transpose(ps_a[:, j * P:(j + 1) * P], oT[:, j * P:(j + 1) * P], ident[:])
                last.then_inc(S["otr_ps"], 1)

            def wait_a(b, what, q):
                if what == "otr" and q == 0:
                    if past(b, 1):
                        pe.wait_ge(S["yT_sb"], b)
                    pe.wait_ge(S["mT_sb"], 2 * b + 2)
                elif what == "otr" and q == 1:
                    if live(b, -1):
                        pe.wait_ge(S["mT_sb"], 2 * b + 3)
                    pe.wait_ge(S["yt_ready"], 4 * b + 1)
                elif what == "otr" and q == 2:
                    pe.wait_ge(S["yt_ready"], 4 * b + 2)
                elif what == "otr" and q == 3:
                    if live(b, -1):
                        pe.wait_ge(S["mT_sb"], 2 * b + 4)
                    pe.wait_ge(S["yt_ready"], 4 * b + 3)

            def m_t(b, g):
                pe.wait_ge(S["m_ready"], 2 * b + 1 + g)
                if g == 1 and (past(b, 1)):
                    pe.wait_ge(S["yt_ready"], 4 * b - 1)
                if g == 1 and not past(b, 1):
                    pe.wait_ge(S["mT_sb"], 1)
                if g == 0 and (past(b, 1)):
                    pe.wait_ge(S["yt_ready"], 4 * b - 3)
                n = GH * TPB
                nc.tensor.transpose(ps_ab[0:3 * n, 0:P], mparts[:].rearrange("p s n -> p (s n)"), identb[:])\
                    .then_inc(S["mT_ps"], 1)

            def project(b, u, t):
                pe.wait_ge(S["xnT_sb"], b + 1)
                if not latent:
                    if t:
                        pe.wait_ge(S["qb_ready"], 2 * b + 1)
                    nc.tensor.matmul(ps_b[:], weff[:, t], xnT[u][:], start=True, stop=True).then_inc(S["q_ps"], 1)
                    return
                if t:
                    pe.wait_ge(S["rope_t"], 2 * b + 1)
                elif past(b, 2):
                    pe.wait_ge(S["v_sb"], b - 1)
                nc.tensor.matmul(ps_b[:], weff[:, t], xnT[u][:], start=True, stop=True)
                nc.tensor.matmul(ps_c[:], weff[:, 3 + t], xnT[u][:], start=True, stop=True).then_inc(S["q_ps"], 1)

            def squares(b, t):
                pe.wait_ge(S["qb_ready"], 2 * b + 1 + t)
                if t:
                    pe.wait_ge(S["floored"], 2 * b + 1)
                elif past(b, 2):
                    pe.wait_ge(S["v_sb"], b - 1)
                nc.tensor.matmul(ps_c[:], ones8[:], sq[:], start=True, stop=True).then_inc(S["sum_ps"], 1)

            kdone = "rope_t" if latent else "floored"

            def slot(i, u, k):
                if k == 0:
                    if live(i):
                        m_t(i, 1)
                    if live(i, 1):
                        pv(i - 1, 1 - u, 3)
                if k == 1:
                    if live(i, 1):
                        otr(i - 1, 3)
                    if live(i, -3):
                        project(i + 3, 1 - u, 0)
                if k == 2:
                    if live(i, 1):
                        pe.wait_ge(S["yt_ready"], 4 * i)
                        for j in range(TPB):
                            last = nc.tensor.transpose(ps_a[:, j * P:(j + 1) * P], yt[:, j].rearrange("p h d -> p (h d)"), ident[:])
                        last.then_inc(S["yT_ps"], 1)
                    if live(i):
                        pv(i, u, 0)
                    if live(i, -3) and not latent:
                        squares(i + 3, 0)
                if k == 3:
                    if live(i):
                        otr(i, 0)
                    if live(i, -3):
                        project(i + 3, 1 - u, 1)
                if k == 4:
                    if live(i, -1):
                        m_t(i + 1, 0)
                    if live(i):
                        pv(i, u, 1)
                    if live(i, -3) and not latent:
                        squares(i + 3, 1)
                if k == 5:
                    if live(i):
                        otr(i, 1)
                    if live(i, 1):
                        pe.wait_ge(S["yT_sb"], i)
                        if live(i, -3):
                            pe.wait_ge(S[kdone], 2 * i + 8)
                        else:
                            pe.wait_ge(S["v_sb"], min(i + 2, B))
                        for j in range(TPB):
                            last = nc.tensor.matmul(ps_c[:, j * P:(j + 1) * P], yT[:, j * P:(j + 1) * P], wc[:], start=True, stop=True)
                        last.then_inc(S["out_ps"], 1)
                if k == 6:
                    if live(i):
                        pv(i, u, 2)
                if k == 7:
                    if live(i):
                        otr(i, 2)
                    if live(i, -2):
                        if live(i, -3):
                            pe.wait_ge(S[kdone], 2 * i + 8)
                        if live(i, 1):
                            pe.wait_ge(S["out_done"], i)
                        for j in range(TPB):
                            last = nc.tensor.matmul(ps_c[:, j * P:(j + 1) * P], xnT[u][:, j * P:(j + 1) * P], weff[:, 2],
                                                    start=True, stop=True)
                        last.then_inc(S["v_ps"], 1)
                    if live(i, -4):
                        xn_t(i + 4)

            def xn_t(b):
                pe.wait_ge(S["xn_ready"], b + 1)
                if past(b, 1):
                    pe.wait_ge(S["rope_t" if latent else "qb_ready"], 2 * b)
                for j in range(TPB):
                    last = nc.tensor.transpose(ps_b[:, j * P:(j + 1) * P], xn[:, j], ident[:])
                last.then_inc(S["xnT_ps"], 1)

            xn_t(0)

            def body(i, u):
                for pair in range(AH // 2):
                    g = pair // 4
                    if pair % 4 == 0:
                        if live(i):
                            pe.wait_ge(mrow[g], 48 * (i + 1))
                        if live(i, -1):
                            pe.wait_ge(load[g], 96 * (i + 2))
                    for k in range(UP):
                        n = UP * pair + k
                        if live(i):
                            s2_unit(i, u, UB * i + n, pair, k)
                        if live(i, -1):
                            s1_unit(i + 1, 1 - u, UB * (i + 1) + n, pair, k)
                    slot(i, u, pair)

            batches(pe, body)

        @block.scalar
        def _(act):
            act.wait_ge(S["zeroed"], 1)
            if not latent:
                act.wait_ge(S["w_in"], 13 * 16)
                act.wait_ge(S["ls_ready"], 1)
                nc.scalar.preload_act_table_set("natural_log_exp_and_others")

            def body(i, u):
                for pair in range(AH // 2):
                    if live(i):
                        for k in range(UP):
                            n = UP * pair + k
                            act.wait_ge(S["s2_ps"], UB * i + n + 1)
                            if n % UQ == 0 and past(4 * i + n // UQ, 2):
                                act.wait_ge(S["pv_ps"], 4 * i + n // UQ - 1)
                            nc.scalar.activation(prob[(n // UQ) % 2][:, n % UQ], ps2[n % 2][:], ACT.Exp, scale=SM)\
                                .then_inc(S["p_sb"], 1)
                    slot(i, u, pair)

            def o_copy(b, q):
                act.wait_ge(S["pv_ps"], 4 * b + q + 1)
                if past(4 * b + q, 1):
                    act.wait_ge(S["otr_ps"], 4 * b + q)
                nc.scalar.copy(oT[:], ps_o[:]).then_inc(S["o_sb"], 1)

            def slot(i, u, k):
                if k == 0 and live(i, 1):
                    o_copy(i - 1, 3)
                if latent and k == 0 and live(i, -1):
                    act.wait_ge(S["v_ps"], i + 2)
                    if live(i, 1):
                        act.wait_ge(S["pv_ps"], 4 * i)
                    nc.scalar.copy(v[1 - u][:, :, :, 0:AD], ps_c[:].rearrange("p (j h d) -> p j h d", j=TPB, h=AH))\
                        .then_inc(S["v_sb"], 1)
                if k == 2 and live(i, 1):
                    act.wait_ge(S["yT_ps"], i)
                    if live(i, 2):
                        act.wait_ge(S["out_ps"], i - 1)
                    nc.scalar.copy(yT[:], ps_a[:]).then_inc(S["yT_sb"], 1)
                if k in (2, 4, 6) and live(i):
                    o_copy(i, k // 2 - 1)
                if k in (1, 3) and live(i, -3) and not latent:
                    biased(i + 3, k // 2)
                if k in (2, 4) and live(i, -3) and not latent:
                    inverse(i + 3, k // 2 - 1)
                if k == 7 and live(i, -4):
                    xnT_copy(i + 4, u)

            def biased(b, t):
                n = 2 * b + t
                act.wait_ge(S["q_ps"], n + 1)
                if past(n, 1):
                    act.wait_ge(S["part_ready"], n)
                    act.wait_ge(S["sum_ps"], n)
                nc.scalar.activation(qb[:], ps_b[:], ACT.Identity, bias=bqk[:, t:t + 1])
                nc.scalar.activation(sq[:], ps_b[:], ACT.Square, bias=bqk[:, t:t + 1]).then_inc(S["qb_ready"], 1)

            def inverse(b, t):
                n = 2 * b + t
                act.wait_ge(S["floored"], n + 1)
                if past(n, 1):
                    act.wait_ge(S["roped"], n)
                nc.scalar.activation(ln[:], t2[:], ACT.Ln).then_inc(S["ln_ready"], 1)
                act.wait_ge(S["ln_ready"], n + 1)
                nc.scalar.activation(t1[:], ln[:], ACT.Exp, scale=-0.5, bias=lsc[:, t:t + 1]).then_inc(S["rope_t"], 1)

            def xnT_copy(b, u):
                act.wait_ge(S["xnT_ps"], b + 1)
                if past(b, 2):
                    act.wait_ge(S["v_ps"], b - 1)
                nc.scalar.copy(xnT[u][:], ps_b[:]).then_inc(S["xnT_sb"], 1)

            xnT_copy(0, 0)
            batches(act, body)

        @block.vector
        def _(dve):
            if latent:
                dve.wait_ge(S["w_in"], 18 * 16)
                nc.vector.memset(up2[:], 0.0).then_inc(S["wrot_ready"], 1)
                dve.wait_ge(S["wrot_ready"], 1)
                for s in range(2):
                    rows = slice(64 * s, 64 * s + 64)
                    nc.vector.tensor_copy(up2[rows, 0:3, s], wup[rows])
                    for t in range(2):
                        e = wup[rows, t, 4:8].rearrange("p (a b) -> p a b", b=2)
                        ro = up2[rows, 3 + t, s, 4:8].rearrange("p (a b) -> p a b", b=2)
                        nc.vector.tensor_scalar(ro[:, :, 0:1], e[:, :, 1:2], -1.0, None, ALU.mult)
                        last = nc.vector.tensor_copy(ro[:, :, 1:2], e[:, :, 0:1])
                last.then_inc(S["wrot_ready"], 1)
                dve.wait_ge(S["weff_ps"], 1)
                nc.vector.tensor_copy(weff[:, 0:4], ps_a[:].rearrange("p (a b) -> p a b", a=4))
                nc.vector.tensor_copy(weff[:, 4], ps_b[:, 0:C]).then_inc(S["weff_ready"], 1)
            else:
                dve.wait_ge(S["w_in"], 13 * 16)
                nc.vector.tensor_scalar(wc[:], wc[:], hsc[:, 0:1], None, ALU.mult).then_inc(S["weff_ready"], 1)
                nc.vector.memset(lsc[:, 0:1], 0.0)
                nc.vector.tensor_scalar(lsc[:, 1:2], lsc[:, 1:2], LOGIT_MAX, None, ALU.min).then_inc(S["ls_ready"], 1)

            def make_xn(b):
                if past(b, 1):
                    dve.wait_ge(S["xnT_ps"], b)
                nc.vector.tensor_tensor(xn[:], y[:, bass.ds(TPB * b, TPB), :],
                                        scale_a[:, bass.ds(TPB * b, TPB)].rearrange("p (n o) -> p n o", o=1).broadcast_to([P, TPB, C]),
                                        ALU.mult).then_inc(S["xn_step"], 1)
                dve.wait_ge(S["xn_step"], b + 1)
                nc.vector.tensor_tensor(xn[:], xn[:],
                                        shift_b[:, bass.ds(TPB * b, TPB)].rearrange("p (n o) -> p n o", o=1).broadcast_to([P, TPB, C]),
                                        ALU.add).then_inc(S["xn_ready"], 1)

            def rope(b, t):
                n = 2 * b + t
                dve.wait_ge(S["q_ps"], n + 1)
                if past(n, 1):
                    dve.wait_ge(S["roped"], n)
                nc.vector.tensor_tensor(t1[:], ps_b[:], cos[:], ALU.mult)
                nc.vector.tensor_tensor(t2[:], ps_c[:], sin[:], ALU.mult).then_inc(S["rope_t"], 1)

            def floor(b, t):
                n = 2 * b + t
                dve.wait_ge(S["sum_ps"], n + 1)
                if past(n, 1):
                    dve.wait_ge(S["rope_t"], n)
                nc.vector.tensor_scalar(t2[:], ps_c[:], NORM_EPS ** 2, None, ALU.max).then_inc(S["floored"], 1)

            def maxima(b, n, pair, k):
                dve.wait_ge(S["s1_ps"], n + 1)
                g, h = pair // 4, (2 * pair) % GH
                bank = ps1[(UP * pair + k) % 2]
                if not latent:
                    last = nc.vector.tensor_reduce(mx[:, g, h + k], bank[:].rearrange("p (a b) -> p a b", a=TPB), X_AX, ALU.max)
                elif k == 4:
                    last = nc.vector.tensor_reduce(mx[:, g, h:h + 2, 1], bank[:].rearrange("p (a b) -> p a b", a=2), X_AX, ALU.max)
                elif k % 2 == 0:
                    last = nc.vector.tensor_reduce(mx[:, g, h + k // 2, 3:4], bank[:], X_AX, ALU.max)
                else:
                    nc.vector.tensor_reduce(mx[:, g, h + k // 2, 2:3], bank[:, 0:384], X_AX, ALU.max)
                    last = nc.vector.tensor_reduce(mx[:, g, h + k // 2, 0:1], bank[:, 384:512], X_AX, ALU.max)
                last.then_inc(S["s1_used"], 1)

            def split(b, g):
                dve.wait_ge(S["s1_used"], UB * b + UB // 2 * (g + 1))
                if past(2 * b + g, 1):
                    dve.wait_ge(S["mT_ps"], 2 * b + g)
                m = mx[:, g].rearrange("p h j -> p (h j)")
                base = 3 * (2 * b + g)
                nc.vector.tensor_copy(mparts[:, 0], m).then_inc(S["m_step"], 1)
                dve.wait_ge(S["m_step"], base + 1)
                nc.vector.tensor_tensor(mres[:], m, mparts[:, 0], ALU.subtract).then_inc(S["m_step"], 1)
                dve.wait_ge(S["m_step"], base + 2)
                nc.vector.tensor_copy(mparts[:, 1], mres[:]).then_inc(S["m_step"], 1)
                dve.wait_ge(S["m_step"], base + 3)
                nc.vector.tensor_tensor(mparts[:, 2], mres[:], mparts[:, 1], ALU.subtract).then_inc(S["m_ready"], 1)

            def m_copy(b, g):
                n = 2 * b + g
                dve.wait_ge(S["mT_ps"], n + 1)
                if past(n, 1):
                    if g == 1:
                        dve.wait_ge(mrow[0], 48 * (b + 1))
                    else:
                        dve.wait_ge(mrow[1], 48 * b)
                nc.vector.tensor_copy(mT[:], ps_ab[0:3 * GH * TPB, 0:P]).then_inc(S["mT_sb"], 1)

            def normalise(b, q):
                n = 4 * b + q
                dve.wait_ge(S["otr_ps"], n + 1)
                o = ps_a[:].rearrange("p (j h d) -> p j h d", j=TPB, h=4)
                nc.vector.reciprocal(rec[:].rearrange("p j (h o) -> p j h o", o=1), o[:, :, :, AD:AD + 1]).then_inc(S["rec_ready"], 1)
                dve.wait_ge(S["rec_ready"], n + 1)
                if q == 0 and (past(b, 1)):
                    dve.wait_ge(S["yT_ps"], b)
                nc.vector.tensor_tensor(yt[:, :, 4 * q:4 * q + 4, :], o[:, :, :, 0:AD],
                                        rec[:].rearrange("p j (h o) -> p j h o", o=1).broadcast_to([P, TPB, 4, AD]), ALU.mult)\
                    .then_inc(S["yt_ready"], 1)

            make_xn(0)

            def slot(i, u, k):
                if k == 0:
                    if live(i):
                        m_copy(i, 1)
                    if live(i, -1) and not latent:
                        dve.wait_ge(S["v_ps"], i + 2)
                        if live(i, 1):
                            dve.wait_ge(S["pv_ps"], 4 * i)
                        nc.vector.tensor_tensor(v[1 - u][:, :, :, 0:AD], ps_c[:].rearrange("p (j h d) -> p j h d", j=TPB, h=AH),
                                                bv[:].rearrange("p o (h d) -> p o h d", h=AH).broadcast_to([P, TPB, AH, AD]),
                                                ALU.add).then_inc(S["v_sb"], 1)
                    if live(i, -4):
                        make_xn(i + 4)
                if k == 1:
                    if live(i, 1):
                        normalise(i - 1, 3)
                    if live(i, -3) and latent:
                        rope(i + 3, 0)
                if k in (2, 4) and live(i, -3) and not latent:
                    floor(i + 3, k // 2 - 1)
                if k == 3:
                    if live(i):
                        normalise(i, 0)
                    if live(i, -3) and latent:
                        rope(i + 3, 1)
                    if live(i, -1):
                        split(i + 1, 0)
                if k == 4:
                    if live(i, -1):
                        m_copy(i + 1, 0)
                if k == 5:
                    if live(i):
                        normalise(i, 1)
                    if live(i, 1):
                        dve.wait_ge(S["out_ps"], i)
                        ys = y[:, bass.ds(TPB * (i - 1), TPB), :]
                        out = ps_c[:].rearrange("p (a b) -> p a b", a=TPB)
                        if latent:
                            nc.vector.tensor_tensor(ys, out, ys, ALU.add).then_inc(S["out_done"], 1)
                        else:
                            nc.vector.tensor_tensor(added[:], out, bo[:].broadcast_to([P, TPB, C]), ALU.add)\
                                .then_inc(S["sum_step"], 1)
                            dve.wait_ge(S["sum_step"], i)
                            nc.vector.tensor_tensor(ys, added[:], ys, ALU.add).then_inc(S["out_done"], 1)
                if k == 7:
                    if live(i):
                        normalise(i, 2)
                    if live(i, -1):
                        split(i + 1, 1)

            def body(i, u):
                for pair in range(AH // 2):
                    if live(i, -1):
                        for k in range(UP):
                            maxima(i + 1, UB * (i + 1) + UP * pair + k, pair, k)
                    slot(i, u, pair)

            batches(dve, body)


E, TOPK, F, SF = 64, 6, 64, 256
CAP = 48
EP = E // 2
PS = 2 * CAP
TW = C + E
HALF = TOK // 2
BIG = 1e30


def moe_shared(nc, tag, rows_of, x, scale_a, shift_b, logits, w, table, xo, ident):
    with ExitStack() as ctx:
        A = Arena(nc, ctx, tag)
        rT = A.sb("rT", [P, E])
        sw1T = A.sb("sw1T", [P, SF])
        sw2T = A.sb("sw2T", [P, 2, C])
        xn = A.sb("xn", [P, TPB, C])
        xnT = A.sb("xnT", [P, T])
        h = A.sb("h", [P, 2, T])
        base = A.sb("base", [P, TPB, C])
        zero = A.sb("zero", [P, C])
        ps_t = A.ps("ps_t", [P, T])
        ps_l = A.ps("ps_l", [P, TPB, E])
        ps_h = [A.ps(f"ps_h{n}", [P, T]) for n in range(2)]
        ps_o = A.ps("ps_o", [P, T])
        S = {n: A.sem(n) for n in ("w_in", "xn_step", "xn_ready", "xn_stored", "xnT_ps", "xnT_sb", "l_ps", "l_sb", "h_ps", "h_sb",
                                   "o_ps", "base_ready", "base_stored", "zeroed", "pad_stored")}
        block = ctx.enter_context(nc.Block())

        def batches(eng, body):
            for i in range(-1, 1):
                body(i)
            with eng.Fori(1, B - 1) as i:
                body(i)
            for i in range(B - 1, B + 1):
                body(i)

        def live(i, lag=0):
            return not isinstance(i, int) or 0 <= i - lag < B

        @block.sync
        def _(sp):
            sp.dma_start(rT[:], w["rT"]).then_inc(S["w_in"], 16)
            sp.dma_start(sw1T[:], w["sw1T"]).then_inc(S["w_in"], 16)
            sp.dma_start(sw2T[:], w["sw2T"].rearrange("(a r) c -> r a c", r=P)).then_inc(S["w_in"], 16)
            sp.wait_ge(S["zeroed"], 1)
            sp.dma_start(xo[TOK:TOK + PS, :], zero[0:PS, :]).then_inc(S["pad_stored"], 16)
            rows = table[0:TOK, 0:C].rearrange(rows_of, p=P)
            outs = xo[0:TOK, :].rearrange(rows_of, p=P)

            def body(i):
                if live(i, -1):
                    sp.wait_ge(S["xn_ready"], i + 2)
                    sp.dma_start(rows[:, bass.ds(TPB * (i + 1), TPB), :], xn[:]).then_inc(S["xn_stored"], 16)
                if live(i, 1):
                    sp.wait_ge(S["base_ready"], i)
                    sp.dma_start(outs[:, bass.ds(TPB * (i - 1), TPB), :], base[:]).then_inc(S["base_stored"], 16)

            batches(sp, body)
            sp.wait_ge(S["xn_stored"], 16 * B)
            sp.wait_ge(S["base_stored"], 16 * B)
            sp.wait_ge(S["pad_stored"], 16)

        @block.gpsimd
        def _(pool):
            nc.gpsimd.memset(zero[:], 0.0).then_inc(S["zeroed"], 1)

        @block.tensor
        def _(pe):
            pe.wait_ge(S["w_in"], 48)

            def body(i):
                if live(i):
                    pe.wait_ge(S["xnT_sb"], i + 1)
                    if past(i, 1):
                        pe.wait_ge(S["l_sb"], i)
                    for j in range(TPB):
                        last = nc.tensor.matmul(ps_l[:, j], xnT[:, j * P:(j + 1) * P], rT[:], start=True, stop=True)
                    last.then_inc(S["l_ps"], 1)
                    for n in range(2):
                        if past(i, 1):
                            pe.wait_ge(S["h_sb"], 2 * i - 1 + n)
                        nc.tensor.matmul(ps_h[n][:], sw1T[:, n * P:(n + 1) * P], xnT[:], start=True, stop=True).then_inc(S["h_ps"], 1)
                if live(i, -1):
                    pe.wait_ge(S["xn_ready"], i + 2)
                    for j in range(TPB):
                        last = nc.tensor.transpose(ps_t[:, j * P:(j + 1) * P], xn[:, j], ident[:])
                    last.then_inc(S["xnT_ps"], 1)
                if live(i):
                    if past(i, 1):
                        pe.wait_ge(S["base_ready"], i)
                    pe.wait_ge(S["h_sb"], 2 * i + 2)
                    for j in range(TPB):
                        for n in range(2):
                            last = nc.tensor.matmul(ps_o[:, j * P:(j + 1) * P], h[:, n, j * P:(j + 1) * P], sw2T[:, n],
                                                    start=n == 0, stop=n == 1)
                    last.then_inc(S["o_ps"], 1)

            batches(pe, body)

        @block.scalar
        def _(act):
            def body(i):
                if live(i):
                    for n in range(2):
                        act.wait_ge(S["h_ps"], 2 * i + 1 + n)
                        if past(i, 1):
                            act.wait_ge(S["o_ps"], i)
                        nc.scalar.activation(h[:, n], ps_h[n][:], ACT.Gelu_apprx_tanh).then_inc(S["h_sb"], 1)
                if live(i, -1):
                    act.wait_ge(S["xnT_ps"], i + 2)
                    if live(i):
                        act.wait_ge(S["h_ps"], 2 * i + 2)
                    nc.scalar.copy(xnT[:], ps_t[:]).then_inc(S["xnT_sb"], 1)

            batches(act, body)

        @block.vector
        def _(dve):
            def make_xn(b):
                if past(b, 1):
                    dve.wait_ge(S["xnT_ps"], b)
                    dve.wait_ge(S["xn_stored"], 16 * b)
                nc.vector.tensor_tensor(xn[:], x[:, bass.ds(TPB * b, TPB), :],
                                        scale_a[:, bass.ds(TPB * b, TPB)].rearrange("p (n o) -> p n o", o=1).broadcast_to([P, TPB, C]),
                                        ALU.mult).then_inc(S["xn_step"], 1)
                dve.wait_ge(S["xn_step"], b + 1)
                nc.vector.tensor_tensor(xn[:], xn[:],
                                        shift_b[:, bass.ds(TPB * b, TPB)].rearrange("p (n o) -> p n o", o=1).broadcast_to([P, TPB, C]),
                                        ALU.add).then_inc(S["xn_ready"], 1)

            def body(i):
                if live(i, -1):
                    make_xn(i + 1)
                if live(i):
                    dve.wait_ge(S["l_ps"], i + 1)
                    nc.vector.tensor_copy(logits[:, bass.ds(TPB * i, TPB), :], ps_l[:]).then_inc(S["l_sb"], 1)
                if live(i, 1):
                    dve.wait_ge(S["o_ps"], i)
                    if past(i, 2):
                        dve.wait_ge(S["base_stored"], 16 * (i - 1))
                    nc.vector.scalar_tensor_tensor(base[:], ps_o[:].rearrange("p (a b) -> p a b", a=TPB), 0.5,
                                                   x[:, bass.ds(TPB * (i - 1), TPB), :], ALU.mult, ALU.add)\
                        .then_inc(S["base_ready"], 1)

            batches(dve, body)


def moe_select(nc, tag, rows_of, logits, w, order_dram, table, lists, ident):
    with ExitStack() as ctx:
        A = Arena(nc, ctx, tag)
        bias = A.sb("bias", [P, 1, E])
        score = A.sb("score", [P, NT, E])
        pick = A.sb("pick", [P, NT, E + 2])
        top = A.sb("top", [P, NT, 8])
        mask = A.sb("mask", [P, NT // 2, 2, E])
        total = A.sb("total", [P, NT])
        order = A.sb("order", [P, HALF])
        val = A.sb("val", [P, HALF])
        first = A.sb("first", [P, CAP])
        cand = A.sb("cand", [E, 2, CAP])
        best = A.sb("best", [E, CAP])
        ps = [A.ps(f"ps{n}", [P, 4, P]) for n in range(4)]
        S = {n: A.sem(n) for n in ("c_in", "score_ready", "step", "mask_ready", "mT_ps", "val_step", "probs_ready", "stored", "best_ready")}
        block = ctx.enter_context(nc.Block())

        @block.sync
        def _(sp):
            sp.dma_start(bias[:], w["bias"].rearrange("(a b e) -> a b e", a=1, b=1).broadcast_to([P, 1, E])).then_inc(S["c_in"], 16)
            sp.dma_start(order[:], order_dram).then_inc(S["c_in"], 16)
            sp.wait_ge(S["probs_ready"], 1)
            sp.dma_start(table[0:TOK, C:TW].rearrange(rows_of, p=P), score[:]).then_inc(S["stored"], 16)
            sp.wait_ge(S["best_ready"], 1)
            sp.dma_start(lists.rearrange("(e s) -> e s", e=E), best[:]).then_inc(S["stored"], 16)
            sp.wait_ge(S["stored"], 32)

        @block.scalar
        def _(act):
            nc.scalar.activation(score[:], logits[:], ACT.Sigmoid).then_inc(S["score_ready"], 1)

        @block.tensor
        def _(pe):
            pe.wait_ge(S["mask_ready"], 1)
            for n in range(NT // 8):
                if n >= 4:
                    pe.wait_ge(S["val_step"], n - 3)
                for j in range(4):
                    t = 4 * n + j
                    last = nc.tensor.transpose(ps[n % 4][:, j], mask[:, t].rearrange("p h e -> p (h e)"), ident[:])
                last.then_inc(S["mT_ps"], 1)

        @block.vector
        def _(dve):
            ch = Chain(dve, S["step"])
            nc.vector.memset(pick[:, :, E:E + 2], BIG)
            dve.wait_ge(S["score_ready"], 1)
            dve.wait_ge(S["c_in"], 32)
            ch.step(nc.vector.tensor_tensor(pick[:, :, 0:E], score[:], bias[:].broadcast_to([P, NT, E]), ALU.add))
            for t in range(NT):
                last = nc.vector.max(top[:, t], pick[:, t])
            ch.step(last)
            for t in range(NT):
                last = nc.vector.match_replace(pick[:, t], top[:, t], pick[:, t], -BIG)
            ch.step(last)
            halves = lambda t: t.rearrange("p (h t) e -> p h t e", h=2)
            mask_h = mask[:].rearrange("p t h e -> p h t e")
            nc.vector.tensor_scalar(mask_h, halves(pick[:])[:, :, :, 0:E], -BIG, None, ALU.is_equal).then_inc(S["mask_ready"], 1)
            dve.wait_ge(S["mask_ready"], 1)
            ch.step(nc.vector.tensor_tensor(halves(score[:]), halves(score[:]), mask_h, ALU.mult))
            ch.step(nc.vector.tensor_reduce(total[:], score[:], X_AX, ALU.add))
            ch.step(nc.vector.tensor_scalar(total[:], total[:], 1e-20, None, ALU.add))
            ch.step(nc.vector.reciprocal(total[:], total[:]))
            nc.vector.tensor_tensor(score[:], score[:], total[:].rearrange("p (n o) -> p n o", o=1).broadcast_to([P, NT, E]),
                                    ALU.mult).then_inc(S["probs_ready"], 1)
            for n in range(NT // 8):
                dve.wait_ge(S["mT_ps"], n + 1)
                nc.vector.tensor_tensor(val[:, 512 * n:512 * n + 512], ps[n % 4][:].rearrange("p a b -> p (a b)"),
                                        order[:, 512 * n:512 * n + 512], ALU.mult).then_inc(S["val_step"], 1)
            dve.wait_ge(S["val_step"], NT // 8)
            for r in range(CAP // 8):
                ch.step(nc.vector.max(first[:, 8 * r:8 * r + 8], val[:]))
                if r < CAP // 8 - 1:
                    ch.step(nc.vector.match_replace(val[:], first[:, 8 * r:8 * r + 8], val[:], 0.0))
            ch.step(nc.vector.tensor_copy(cand[:, 0], first[0:E, :]))
            ch.step(nc.vector.tensor_copy(cand[:, 1], first[E:2 * E, :]))
            cand2 = cand[:].rearrange("p a b -> p (a b)")
            for r in range(CAP // 8):
                ch.step(nc.vector.max(best[:, 8 * r:8 * r + 8], cand2))
                if r < CAP // 8 - 1:
                    ch.step(nc.vector.match_replace(cand2, best[:, 8 * r:8 * r + 8], cand2, 0.0))
            nc.vector.tensor_scalar(best[:], best[:], -1.0, float(TOK), ALU.mult, ALU.add).then_inc(S["best_ready"], 1)


def moe_experts(nc, tag, w, table, lists, xo, ident):
    with ExitStack() as ctx:
        A = Arena(nc, ctx, tag)
        w1 = A.sb("w1", [P, E, F])
        w2 = A.sb("w2", [P, EP, C])
        lp = A.sb("lp", [EP, PS])
        tb = A.sb("tb", [PS, EP, PS])
        tok = A.sb("tok", [PS, EP])
        own = A.sb("own", [PS, 2])
        later = A.sb("later", [PS, PS])
        dummy = A.sb("dummy", [PS, 1])
        gidx_f = A.sb("gidx_f", [PS, EP])
        gidx = A.sb("gidx", [PS, EP], U32)
        sidx_f = A.sb("sidx_f", [PS, EP])
        sidx = A.sb("sidx", [PS, EP], U32)
        same = A.sb("same", [PS, EP, PS])
        tmp = A.sb("tmp", [PS, EP, PS])
        dup = A.sb("dup", [PS, EP])
        inv = A.sb("inv", [PS, EP])
        wt = A.sb("wt", [PS, EP])
        xs = A.sb("xs", [PS, EP, TW])
        xsT = A.sb("xsT", [P, EP, PS])
        hb = A.sb("hb", [P, EP, PS])
        ys = A.sb("ys", [PS, EP, C])
        yc = A.sb("yc", [PS, EP, C])
        ps_t = [A.ps(f"ps_t{n}", [P, 512]) for n in range(2)]
        ps_h = [A.ps(f"ps_h{n}", [P, 512]) for n in range(2)]
        ps_y = [A.ps(f"ps_y{n}", [P, 4, C]) for n in range(2)]
        ps_c = [A.ps(f"ps_c{n}", [P, 4, C]) for n in range(2)]
        S = {n: A.sem(n) for n in ("w_in", "c_in", "lp_in", "tb_in", "tok_ps", "step", "gidx_ready", "sidx_ready", "gathered", "zeroed",
                                   "xs_ps", "xs_sb", "h_ps", "h_sb", "wt_ready", "y_ps", "y_sb", "same_ready", "c_ps", "c_sb",
                                   "scattered")}
        G4 = EP // 4
        block = ctx.enter_context(nc.Block())

        @block.sync
        def _(sp):
            sp.dma_start(lp[:], lists.rearrange("(c s) -> c s", c=EP)).then_inc(S["lp_in"], 16)
            sp.dma_start(tb[:], lists.rearrange("(a c s) -> a c s", a=1, c=EP).broadcast_to([PS, EP, PS])).then_inc(S["tb_in"], 16)
            sp.dma_start(own[:], w["own"]).then_inc(S["c_in"], 16)
            sp.dma_start(later[:], w["later"]).then_inc(S["c_in"], 16)
            sp.dma_start(dummy[:], w["spare"]).then_inc(S["c_in"], 16)
            sp.dma_start(w1[:], w["w1"].rearrange("e c f -> c e f")).then_inc(S["w_in"], 16)
            sp.dma_start(w2[:], w["w2"].rearrange("(a s) f c -> (s f) a c", s=2)).then_inc(S["w_in"], 16)

        @block.gpsimd
        def _(pool):
            nc.gpsimd.memset(hb[:], 0.0).then_inc(S["zeroed"], 1)
            pool.wait_ge(S["gidx_ready"], 1)
            for c in range(EP):
                nc.gpsimd.indirect_dma_start(out=xs[:, c, :], out_offset=None, in_=table[:, :],
                                             in_offset=bass.IndirectOffsetOnAxis(ap=gidx[:, c:c + 1], axis=0))\
                    .then_inc(S["gathered"], 16)
            pool.wait_ge(S["sidx_ready"], 1)
            for c in range(EP):
                pool.wait_ge(S["c_sb"], c // 4 + 1)
                if c:
                    pool.wait_ge(S["scattered"], 16 * c)
                nc.gpsimd.indirect_dma_start(out=xo[:, :], out_offset=bass.IndirectOffsetOnAxis(ap=sidx[:, c:c + 1], axis=0),
                                             in_=yc[:, c, :], in_offset=None, compute_op=ALU.add,
                                             bounds_check=TOK + PS - 1, oob_is_err=True)\
                    .then_inc(S["scattered"], 16)
            pool.wait_ge(S["scattered"], 16 * EP)

        @block.tensor
        def _(pe):
            pe.wait_ge(S["lp_in"], 16)
            nc.tensor.transpose(ps_y[0][0:PS, 0, 0:EP], lp[:], ident[0:EP, 0:EP]).then_inc(S["tok_ps"], 1)
            pe.wait_ge(S["w_in"], 32)
            for g in range(G4):
                pe.wait_ge(S["gathered"], 16 * EP) if g == 0 else None
                if g >= 2:
                    pe.wait_ge(S["xs_sb"], g - 1)
                for j in range(4):
                    last = nc.tensor.transpose(ps_t[g % 2][:, PS * j:PS * j + PS], xs[:, 4 * g + j, 0:C], ident[0:PS, 0:PS])
                last.then_inc(S["xs_ps"], 1)
            for g in range(G4 + 1):
                if g < G4:
                    pe.wait_ge(S["xs_sb"], g + 1)
                    if g >= 2:
                        pe.wait_ge(S["h_sb"], g - 1)
                    for j in range(4):
                        for s in range(2):
                            c = 4 * g + j
                            last = nc.tensor.matmul(ps_h[g % 2][64 * s:64 * s + 64, CAP * j:CAP * j + CAP], w1[:, 2 * c + s, :],
                                                    xsT[:, c, CAP * s:CAP * s + CAP], start=True, stop=True)
                    last.then_inc(S["h_ps"], 1)
                if g:
                    pe.wait_ge(S["h_sb"], g)
                    if g == 1:
                        pe.wait_ge(S["gidx_ready"], 1)
                    if g >= 3:
                        pe.wait_ge(S["y_sb"], g - 2)
                    for j in range(4):
                        c = 4 * (g - 1) + j
                        last = nc.tensor.matmul(ps_y[(g - 1) % 2][0:PS, j], hb[:, c], w2[:, c], start=True, stop=True)
                    last.then_inc(S["y_ps"], 1)
            pe.wait_ge(S["same_ready"], 1)
            for g in range(G4):
                pe.wait_ge(S["y_sb"], g + 1)
                if g >= 2:
                    pe.wait_ge(S["c_sb"], g - 1)
                for j in range(4):
                    c = 4 * g + j
                    last = nc.tensor.matmul(ps_c[g % 2][0:PS, j], same[:, c], ys[:, c], start=True, stop=True)
                last.then_inc(S["c_ps"], 1)

        @block.scalar
        def _(act):
            act.wait_ge(S["zeroed"], 1)
            for g in range(G4):
                act.wait_ge(S["xs_ps"], g + 1)
                nc.scalar.copy(xsT[:, 4 * g:4 * g + 4], ps_t[g % 2][:, 0:4 * PS].rearrange("p (a b) -> p a b", a=4)).then_inc(S["xs_sb"], 1)
            for g in range(G4):
                act.wait_ge(S["h_ps"], g + 1)
                for s in range(2):
                    last = nc.scalar.activation(hb[64 * s:64 * s + 64, 4 * g:4 * g + 4, CAP * s:CAP * s + CAP],
                                                ps_h[g % 2][64 * s:64 * s + 64, 0:4 * CAP].rearrange("p (a b) -> p a b", a=4),
                                                ACT.Gelu_apprx_tanh)
                last.then_inc(S["h_sb"], 1)
            for g in range(G4):
                act.wait_ge(S["c_ps"], g + 1)
                nc.scalar.copy(yc[:, 4 * g:4 * g + 4], ps_c[g % 2][0:PS]).then_inc(S["c_sb"], 1)

        @block.vector
        def _(dve):
            ch = Chain(dve, S["step"])
            dve.wait_ge(S["tok_ps"], 1)
            ch.step(nc.vector.tensor_copy(tok[:], ps_y[0][0:PS, 0, 0:EP]))
            ch.step(nc.vector.tensor_scalar(gidx_f[:], tok[:], float(TOK - 1), None, ALU.min))
            nc.vector.tensor_copy(gidx[:], gidx_f[:]).then_inc(S["gidx_ready"], 1)
            ch.step(nc.vector.tensor_scalar(inv[:], tok[:], float(TOK), None, ALU.is_equal))
            dve.wait_ge(S["tb_in"], 16)
            dve.wait_ge(S["c_in"], 48)
            nc.vector.tensor_tensor(same[:], tb[:], tok[:].rearrange("p (c o) -> p c o", o=1).broadcast_to([PS, EP, PS]),
                                    ALU.is_equal).then_inc(S["same_ready"], 1)
            dve.wait_ge(S["same_ready"], 1)
            ch.step(nc.vector.tensor_tensor(tmp[:], same[:], later[:].rearrange("p (o k) -> p o k", o=1).broadcast_to([PS, EP, PS]),
                                            ALU.mult))
            ch.step(nc.vector.tensor_reduce(dup[:], tmp[:], X_AX, ALU.max))
            ch.step(nc.vector.tensor_tensor(dup[:], dup[:], inv[:], ALU.max))
            ch.step(nc.vector.tensor_scalar(sidx_f[:], tok[:], -1.0, dummy[:, 0:1], ALU.mult, ALU.add))
            ch.step(nc.vector.tensor_tensor(sidx_f[:], sidx_f[:], dup[:], ALU.mult))
            ch.step(nc.vector.tensor_tensor(sidx_f[:], sidx_f[:], tok[:], ALU.add))
            nc.vector.tensor_copy(sidx[:], sidx_f[:]).then_inc(S["sidx_ready"], 1)
            ch.step(nc.vector.tensor_scalar(inv[:], inv[:], -0.5, 0.5, ALU.mult, ALU.add))
            dve.wait_ge(S["gathered"], 16 * EP)
            pair_w = xs[:, :, C:TW]
            for c in range(EP):
                last = nc.vector.tensor_tensor(tmp[:, c, 0:2], pair_w[:, c, 2 * c:2 * c + 2], own[:], ALU.mult)
            ch.step(last)
            ch.step(nc.vector.tensor_reduce(wt[:], tmp[:, :, 0:2], X_AX, ALU.add))
            ch.step(nc.vector.tensor_tensor(wt[:], wt[:], inv[:], ALU.mult))
            for g in range(G4):
                dve.wait_ge(S["y_ps"], g + 1)
                nc.vector.tensor_tensor(ys[:, 4 * g:4 * g + 4], ps_y[g % 2][0:PS],
                                        wt[:, 4 * g:4 * g + 4].rearrange("p (c o) -> p c o", o=1).broadcast_to([PS, 4, C]),
                                        ALU.mult).then_inc(S["y_sb"], 1)


TILES = "(n p) c -> p n c"
RUNS = "(p n) c -> p n c"


def load_tokens(nc, tag, dst, src, rows_of, extra=()):
    with ExitStack() as ctx:
        A = Arena(nc, ctx, tag)
        loaded = A.sem("loaded")
        block = ctx.enter_context(nc.Block())

        @block.sync
        def _(sp):
            sp.dma_start(dst[:], src[0:TOK, :].rearrange(rows_of, p=P)).then_inc(loaded, 16)
            for t, d in extra:
                sp.dma_start(t[:], d).then_inc(loaded, 16)
            sp.wait_ge(loaded, 16 * (1 + len(extra)))


def routed_ffn(nc, tag, x, y, a, b, logk, w, s_scr, ident, iota):
    with ExitStack() as ctx:
        A = Arena(nc, ctx, tag)
        s_rows = A.sb("s_rows", [ROWS, T])
        scores = A.sb("scores", [ROWS, T])
        posw = A.sb("posw", [P, 2, TPB, ROWS])
        router_prologue(nc, tag + "r", x, a, b, s_rows, s_scr, w["rtok"], ident)
        light_attention(nc, tag + "l", x, y, a, b, s_rows, scores, logk,
                        dict(wq=w["wq_light"], wkv=w["wkv_light"], wo=w["wo_light"], gamma=w["gamma_light"]), ident)
        route_tokens(nc, tag + "t", scores, posw, ident)
        heavy_attention(nc, tag + "h", x, y, a, b, posw,
                        dict(wq=w["wq_heavy"], wkvT=w["wkvT_heavy"], wo=w["wo_heavy"], gamma=w["gamma_heavy"]), ident, iota)


def macaron_block(nc, w, out):
    scratch = nc.dram_tensor("stack_parts", (2, 3, AD, AH, T), BF16).ap()
    s_scr = nc.dram_tensor("router_scores", (P, P), F32).ap()
    table = nc.dram_tensor("gather_table", (TOK, TW), F32).ap()
    lists = nc.dram_tensor("expert_tokens", (E * CAP,), F32).ap()
    mid = nc.dram_tensor("x_after_experts", (TOK + PS, C), F32).ap()
    with ExitStack() as ctx:
        A = Arena(nc, ctx, "g")
        ident = A.sb("ident", [P, P])
        identb = A.sb("identb", [P, P], BF16)
        iota = A.sb("iota", [P, NKV])
        logk = A.sb("logk", [ROWS, 1])
        a = A.sb("a", [P, NT])
        b = A.sb("b", [P, NT])
        y = A.sb("y", [P, NT, C])
        with nc.Block() as block:
            @block.gpsimd
            def _(pool):
                nc.gpsimd.memset(logk[0:KV0, :], float(np.log(np.float32(min(NQ * FETCH, T)))))
                nc.gpsimd.memset(logk[KV0:ROWS, :], float(np.log(np.float32(min(NKV * FETCH, T)))))
        with ExitStack() as inner:
            x = Arena(nc, inner, "g1").sb("x", [P, NT, C])
            load_tokens(nc, "ld1", x, w["x"], TILES, [(ident, w["ident"]), (identb, w["identb"]), (iota, w["iota"])])
            routed_ffn(nc, "f1", x, y, a, b, logk, w, s_scr, ident, iota)
        stacked_attention(nc, "la", True, y, a, b, w, scratch, ident, identb)
        with ExitStack() as inner:
            x = Arena(nc, inner, "g2").sb("x", [P, NT, C])
            routed_ffn(nc, "f2", y, x, a, b, logk, w, s_scr, ident, iota)
            norm_stats(nc, "n2", x, a, b)
            logits = Arena(nc, inner, "g3").sb("logits", [P, NT, E])
            moe_shared(nc, "s1", TILES, x, a, b, logits, w, table, mid, ident)
            moe_select(nc, "e1", TILES, logits, w, w["order_tiles"], table, lists, ident)
        moe_experts(nc, "m1", w, table, lists, mid, ident)
        load_tokens(nc, "ld2", y, mid, RUNS)
        stacked_attention(nc, "ca", False, y, a, b, w, scratch, ident, identb)
        norm_stats(nc, "n4", y, a, b)
        with ExitStack() as inner:
            logits = Arena(nc, inner, "g4").sb("logits", [P, NT, E])
            moe_shared(nc, "s2", RUNS, y, a, b, logits, w, table, out, ident)
            moe_select(nc, "e2", RUNS, logits, w, w["order_runs"], table, lists, ident)
        moe_experts(nc, "m2", w, table, lists, out, ident)


def shape_constants():
    bf16 = mybir.dt.np(BF16)
    half = AD // 2
    inv = (1.0 / np.float32(10000.0) ** (np.arange(0, half, 2, dtype=np.float32) / np.float32(half))).astype(np.float32)
    freqs = np.arange(T, dtype=np.float32)[:, None] * inv[None]
    angles = np.concatenate([freqs, freqs], -1)
    cos = np.ones((AH, AD, T), np.float32)
    sin = np.zeros((AH, AD, T), np.float32)
    cos[:, half:] = np.cos(angles).T
    sin[:, half:] = np.sin(angles).T
    p = np.arange(P)
    maskq = np.where(p[None, :] > p[:, None], -BIG, 0).astype(bf16)
    own8 = np.arange(T)[None, :] % 8 == np.arange(8)[:, None]
    tile = np.arange(NT)
    tiles, runs = (np.repeat((TOK - t).reshape(2, HALF).astype(np.float32), E, axis=0)
                   for t in (tile[:, None] * P + p[None], p[None] * NT + tile[:, None]))
    own = np.zeros((PS, 2), np.float32)
    own[:CAP, 0] = own[CAP:, 1] = 1
    later = np.zeros((PS, PS), np.float32)
    later[CAP:, :CAP] = 1
    return dict(
        ident=np.eye(P, dtype=np.float32), identb=np.eye(P, dtype=bf16), iota=np.tile(np.arange(NKV, dtype=np.float32), (P, 1)),
        cos=cos.reshape(P, T), sin=sin.reshape(P, T), maskq=maskq, maskk=np.ascontiguousarray(maskq.T),
        ones8=(p[:, None] // AD == p[None] // AD).astype(np.float32),
        block_rows=np.stack([np.where(own8, -BIG, 0), np.where(own8, 0, 1)]).astype(bf16),
        order_tiles=tiles, order_runs=runs, own=own, later=later,
        spare=(TOK + np.arange(PS, dtype=np.float32)).reshape(PS, 1))


def kernel(**inputs):
    import concourse.bacc as bacc
    from concourse.bass_utils import run_bass_kernel_spmd

    get = lambda name: np.ascontiguousarray(np.asarray(inputs[name]))
    turn = lambda name: np.ascontiguousarray(np.asarray(inputs[name]).T)
    f, l, c, m = "L0_ffn_", "L0_attn_", "L1_attn_", "L1_ffn_"
    arrays = dict(
        x=get("L0_attn_x").reshape(TOK, C),
        wq_light=get(f + "wq_light"), wkv_light=get(f + "wkv_light"), wo_light=get(f + "wo_light"), gamma_light=get(f + "gamma_light"),
        wq_heavy=get(f + "wq_heavy"), wkvT_heavy=turn(f + "wkv_heavy"), wo_heavy=get(f + "wo_heavy"), gamma_heavy=get(f + "gamma_heavy"),
        rtok=np.stack([get(f + "q_routing_token"), get(f + "kv_routing_token")]),
        qdT=turn(l + "Wq_down"), kdT=turn(l + "Wk_down"), vdT=turn(l + "Wv_down"),
        qc=get(l + "Wq_up_c"), qe=get(l + "Wq_up_e"), kc=get(l + "Wk_up_c"), ke=get(l + "Wk_up_e"), vu=get(l + "Wv_up"), wc=get(l + "Wc"),
        winT=turn(c + "in_proj_weight"), woT=turn(c + "out_w"), bin=get(c + "in_proj_bias"), bo=get(c + "out_b"),
        ls=np.repeat(get(c + "logit_scale").reshape(AH), AD), hs=np.repeat(get(c + "head_scale").reshape(AH), AD),
        rT=turn(m + "router_weight"), bias=get(m + "expert_bias"), w1=get(m + "w1"), w2=get(m + "w2"),
        sw1T=turn(m + "sw1"), sw2T=turn(m + "sw2"), **shape_constants())
    nc = bacc.Bacc("TRN2", target_bir_lowering=False, num_devices=1)
    w = {n: nc.dram_tensor(f"in_{n}", v.shape, mybir.dt.from_np(v.dtype), kind="ExternalInput").ap() for n, v in arrays.items()}
    out = nc.dram_tensor("out_x", (TOK + PS, C), F32, kind="ExternalOutput").ap()
    macaron_block(nc, w, out)
    r = run_bass_kernel_spmd(nc, [{f"in_{n}": v for n, v in arrays.items()}], core_ids=[0])
    return r.results[0]["out_x"][:TOK].reshape(B, T, C)
```
